# Optimizing a Trainium2 kernel written in Bass

```python
import numpy as np
import jax
import jax.numpy as jnp

def _softmax(x, axis=-1):
    return jax.nn.softmax(x, axis=axis)
def _gelu(x):
    return jax.nn.gelu(x, approximate=True)
def _silu(x):
    return jax.nn.silu(x)
def _sigmoid(x):
    return jax.nn.sigmoid(x)
def _layernorm(x, axis=-1, eps=1e-5):
    m = jnp.mean(x, axis=axis, keepdims=True)
    v = jnp.var(x, axis=axis, keepdims=True)
    return (x - m) / jnp.sqrt(v + eps)
def _scatter_add(tgt, idx, src, axis=0):
    return tgt.at[idx].add(src)
def _segment_sum(src, seg, n):
    return jax.ops.segment_sum(src, seg, n)

kernel_name = 'mk_adj_preln_d2_adj_128_77babb'

def setup_inputs(seed: int = 0):
    np.random.seed(seed)
    _w = jnp.asarray
    def _rec_inputs():
        import jax
        import jax.numpy as jnp
        _gk = jax.random.key(seed)
        x = 7.22e-05 + 1 * jax.random.normal(jax.random.fold_in(_gk, 1), (8, 2048, 128), jnp.float32)
        _a = jax.random.bernoulli(jax.random.fold_in(_gk, 2), 0.0078125, (2048, 2048))
        _a = jnp.logical_or(_a, jnp.swapaxes(_a, -1, -2))
        _a = jnp.logical_or(_a, jnp.eye(2048, dtype=bool))
        _af = _a.astype(jnp.float32)
        _af = _af * jax.random.uniform(jax.random.fold_in(_gk, 3), (2048, 2048), jnp.float32, 0.05, 0.000976562)
        adj = _af
        return x, adj
    x, adj = _rec_inputs()
    def _L0_gnn_setup():
        import jax, jax.numpy as jnp
        import numpy as np
        B, N, F_IN, F_OUT, ORDERS = (32, 2048, 128, 128, 2)
        NUM_MATRICES = 2 * ORDERS + 1

        def _cheb_hops(x0, A, orders):
            hops = []
            x1 = jnp.einsum('bnf,nw->bwf', x0, A)
            hops.append(x1)
            xk_1, xk_2 = (x1, x0)
            for _ in range(2, orders + 1):
                x2 = 2.0 * jnp.einsum('bnf,nw->bwf', xk_1, A) - xk_2
                hops.append(x2)
                xk_1, xk_2 = (x2, xk_1)
            return hops
        key = jax.random.key(seed)
        k1, k2, k3, k4, k5 = jax.random.split(key, 5)
        X = jax.random.normal(k1, (B, N, F_IN), dtype=jnp.float32)
        A1 = jax.random.uniform(k2, (N, N), dtype=jnp.float32) * (2.0 / N)
        A2 = jax.random.uniform(k3, (N, N), dtype=jnp.float32) * (2.0 / N)
        stdv = 1.0 / np.sqrt(F_OUT)
        Theta1 = jax.random.uniform(k4, (F_IN * NUM_MATRICES, F_OUT), dtype=jnp.float32, minval=-stdv, maxval=stdv)
        bias = jax.random.uniform(k5, (F_OUT,), dtype=jnp.float32, minval=-stdv, maxval=stdv)
        return {'X': X, 'A1': A1, 'A2': A2, 'Theta1': Theta1, 'bias': bias}
    _L0_gnn_all = _L0_gnn_setup()
    _L0_gnn_in = {k: v for k, v in _L0_gnn_all.items() if k in ('Theta1', 'bias', )}
    del _L0_gnn_all

    def _L1_gnn_setup():
        import jax, jax.numpy as jnp
        import numpy as np
        B, N, F_IN, F_OUT = (4, 4096, 128, 128)
        NEG_SLOPE = 0.2
        EDGE_PROB = 0.05
        key = jax.random.key(seed)
        kx, ka, kw, ks, kd = jax.random.split(key, 5)
        x = jax.random.normal(kx, (B, N, F_IN), dtype=jnp.float32)
        a = (jax.random.uniform(ka, (N, N)) < EDGE_PROB).astype(jnp.float32)
        a = a.at[jnp.arange(N), jnp.arange(N)].set(1.0)
        bw = float(np.sqrt(6.0 / (F_IN + F_OUT)))
        w = jax.random.uniform(kw, (F_IN, F_OUT), minval=-bw, maxval=bw, dtype=jnp.float32)
        ba = float(np.sqrt(6.0 / (1 + F_OUT)))
        a_src = jax.random.uniform(ks, (F_OUT,), minval=-ba, maxval=ba, dtype=jnp.float32)
        a_dst = jax.random.uniform(kd, (F_OUT,), minval=-ba, maxval=ba, dtype=jnp.float32)
        return {'x': x, 'a': a, 'w': w, 'a_src': a_src, 'a_dst': a_dst}
    _L1_gnn_all = _L1_gnn_setup()
    _L1_gnn_in = {k: v for k, v in _L1_gnn_all.items() if k in ('w', 'a_src', 'a_dst', )}
    del _L1_gnn_all

    return {
        "x": x,
        "adj": adj,
        "L0_gnn_Theta1": _L0_gnn_in["Theta1"],
        "L0_gnn_bias": _L0_gnn_in["bias"],
        "L1_gnn_w": _L1_gnn_in["w"],
        "L1_gnn_a_src": _L1_gnn_in["a_src"],
        "L1_gnn_a_dst": _L1_gnn_in["a_dst"],
    }

def reference(x, adj, L0_gnn_Theta1, L0_gnn_bias, L1_gnn_w, L1_gnn_a_src, L1_gnn_a_dst):
    import jax
    import jax.numpy as jnp
    def _L0_gnn_ref(X, A1, A2, Theta1, bias):
        import jax, jax.numpy as jnp
        import numpy as np
        B, N, F_IN, F_OUT, ORDERS = (32, 2048, 128, 128, 2)
        NUM_MATRICES = 2 * ORDERS + 1

        def _cheb_hops(x0, A, orders):
            hops = []
            x1 = jnp.einsum('bnf,nw->bwf', x0, A)
            hops.append(x1)
            xk_1, xk_2 = (x1, x0)
            for _ in range(2, orders + 1):
                x2 = 2.0 * jnp.einsum('bnf,nw->bwf', xk_1, A) - xk_2
                hops.append(x2)
                xk_1, xk_2 = (x2, xk_1)
            return hops
        xs = [X] + _cheb_hops(X, A1, ORDERS) + _cheb_hops(X, A2, ORDERS)
        x = jnp.stack(xs, axis=2)
        b, n = (X.shape[0], X.shape[1])
        x = x.reshape(b, n, -1)
        out = jax.nn.relu(x @ Theta1 + bias)
        return out

    def _L1_gnn_ref(x, a, w, a_src, a_dst):
        import jax, jax.numpy as jnp
        import numpy as np
        B, N, F_IN, F_OUT = (4, 4096, 128, 128)
        NEG_SLOPE = 0.2
        EDGE_PROB = 0.05
        h = jnp.einsum('bnf,fo->bno', x, w)
        e_src = jnp.einsum('bno,o->bn', h, a_src)
        e_dst = jnp.einsum('bno,o->bn', h, a_dst)
        e = jax.nn.leaky_relu(e_src[:, :, None] + e_dst[:, None, :], negative_slope=NEG_SLOPE)
        mask = (a > 0)[None, :, :]
        e = jnp.where(mask, e, -jnp.inf)
        alpha = jax.nn.softmax(e, axis=-1)
        out = jnp.einsum('bij,bjo->bio', alpha, h)
        return out

    h = jnp.maximum(_layernorm(x, axis=-1), 0.0)
    x = x + _L0_gnn_ref(h, adj, adj, L0_gnn_Theta1, L0_gnn_bias)
    h = jnp.maximum(_layernorm(x, axis=-1), 0.0)
    x = x + _L1_gnn_ref(h, adj, L1_gnn_w, L1_gnn_a_src, L1_gnn_a_dst)
    return x


_drawn_inputs = setup_inputs


def setup_inputs(seed=0):
    import zlib

    import numpy as np

    out = dict(_drawn_inputs(seed))
    spreads = {}
    factors = {}
    for name, (base, spread) in spreads.items():
        noise = np.random.default_rng([zlib.crc32(name.encode()), seed]).standard_normal(out[name].shape)
        drawn = base * np.exp(spread * noise) if base else spread * noise
        out[name] = jnp.asarray(drawn.astype(out[name].dtype))
    for name, factor in factors.items():
        out[name] = (out[name] * factor).astype(out[name].dtype)
    return out
```

```python
import concourse.bass as bass
from concourse import mybir
from contextlib import ExitStack

F32 = mybir.dt.float32
F32R = mybir.dt.float32r
BF16 = mybir.dt.bfloat16
ALU = mybir.AluOpType
ACT = mybir.ActivationFunctionType
AX = mybir.AxisListType
RMAX = bass.bass_isa.ReduceOp.max

P = 128
B, N, D = 8, 2048, 128
HB = B // 2
W = HB * D
NT = N // P
Q = 4
KQ = NT // Q
EPS = 1e-5
SLOPE = 0.2
GC = D + 1
DMA = 16
UNTIL = NT // 2


def wait_alone(eng, sem, value, passed):
    eng.wait_ge(sem, value)
    eng.sem_inc(passed, 1)


def layer0(nc, pad_dram, x, adj, theta, bias, gw, a_src, a_dst, z_dram, mt_dram, x1_dram, g_dram, s_dram):
    ctx = ExitStack()
    with ctx:
        def sb(name, shape, dt=F32):
            return ctx.enter_context(nc.sbuf_tensor(name, shape, dt))

        def sem(name):
            return ctx.enter_context(nc.semaphore(name))

        z_hi = sb("z_hi", [P, NT, W], F32R)
        z_lo = sb("z_lo", [P, NT, W], F32R)
        u_hi = sb("u_hi", [P, NT, W], F32R)
        u_lo = sb("u_lo", [P, NT, W], F32R)
        xh = sb("xh", [P, NT, HB, D])
        a_raw = sb("a_raw", [P, Q, KQ * P])
        a_hi = sb("a_hi", [P, Q, KQ, P], F32R)
        a_lo = sb("a_lo", [P, Q, KQ, P], F32R)
        ring = sb("ring", [P, 4, W])
        stage = sb("stage", [P, 2, HB * GC])
        mask = sb("mask", [P, 2, KQ * P], BF16)
        mask_t = sb("mask_t", [P, 2, KQ * P], BF16)
        row_st = mask_t[0:1, :, :].rearrange("p e c -> p (e c)").bitcast(F32)
        ident = sb("ident", [P, P])
        ident16 = sb("ident16", [P, P], BF16)
        t_cat = sb("t_cat", [P, 3, D])
        bias_b = sb("bias_b", [P, D])
        w_ext = sb("w_ext", [P, GC + 1])
        bst = sb("bst", [P, NT * HB, 6])
        st = sb("st", [P, 6, NT * HB])
        eps_t = sb("eps_t", [P, 1])
        MSUM, DIFF, M2, SQ, VAR, SD = range(6)
        RSTD, NMR = DIFF, M2
        ps = ctx.enter_context(nc.psum_tensor("ps", [P, 8, 512], F32))
        acc = [ps[:, s, :] for s in range(2)]
        ps_m = [ps[:, 2 + e, 0:KQ * P // 2].bitcast(BF16) for e in range(2)]
        ps_t = [ps[:, 4 + s, :] for s in range(2)]
        ps_z2 = [ps[:, 6 + s, :] for s in range(2)]
        ps_z10 = [ps[:, 2 * s:2 * s + 2, :] for s in range(2)]
        ps_g = [ps[:, 2 * s:2 * s + 2, 0:2 * GC] for s in range(2)]
        ps_row = [ps[0:1, 6 + s, :] for s in range(2)]
        th = ring[:, :, :].rearrange("p a w -> p (a w)")[:, 0:5 * D].rearrange("p (m d) -> p m d", m=5)
        w_t = stage[:, 0, 0:D]
        a_cols = stage[:, 0, D:D + 2]

        passed = sem("passed")
        par_in = sem("par_in")
        ident_ready = sem("ident_ready")
        set_up = sem("set_up")
        w_done = sem("w_done")
        x_in = [sem(f"x_in{g}") for g in range(4)]
        stats_done = sem("stats_done")
        norm_step = sem("norm_step")
        var_ready = sem("var_ready")
        sd_ready = sem("sd_ready")
        norm_ready = sem("norm_ready")
        h_ready = sem("h_ready")
        transposed = sem("transposed")
        ht_ready = sem("ht_ready")
        projected = sem("projected")
        evacuated = sem("evacuated")
        zhi_done = sem("zhi_done")
        z_staged = sem("z_staged")
        row_staged = sem("row_staged")
        stage_out = [sem(f"stage_out{s}") for s in range(2)]
        row_out = sem("row_out")
        a_in = [sem(f"a_in{q}") for q in range(Q)]
        hi_ready = sem("hi_ready")
        split_ready = sem("split_ready")
        chunk_used = sem("chunk_used")
        zin = [sem(f"zin{s}") for s in range(2)]
        summed = sem("summed")
        uhi_done = sem("uhi_done")
        u_ready = sem("u_ready")
        x1_ready = sem("x1_ready")
        x1_out = sem("x1_out")
        mask_ready = sem("mask_ready")
        mask_turned = sem("mask_turned")
        mask_copied = sem("mask_copied")
        mask_out = [sem(f"mask_out{e}") for e in range(2)]

        x_v = x.rearrange("(h b) (t p) f -> h t p b f", b=HB, p=P)
        adj_v = adj.rearrange("(k p) (w c) -> w p k c", p=P, c=P)

        def v_of(half, phase, i, s):
            return half * (2 * NT) + (phase * NT + s) + i * 2

        TURNED, REST, HOP2 = 0, UNTIL, NT

        def n_of(half, first, i, s=0):
            return half * (2 * NT) + (first + s) + i * 2

        def w_of(half, first, i, s=0):
            if first == TURNED:
                return half * UNTIL + i * 2 + s
            if first == REST:
                return (UNTIL - half * UNTIL) + i * 2 + s
            return i * 2 + s

        block = ctx.enter_context(nc.Block())

        @block.sync
        def _(sp):
            for m in range(5):
                sp.dma_start(th[:, m, :], theta[m * D:(m + 1) * D, :]).then_inc(par_in, DMA)
            sp.dma_start(w_ext[:, 0:D], gw).then_inc(par_in, DMA)
            sp.dma_start(a_cols[:, 0:1], a_dst.rearrange("(f a) -> f a", a=1)).then_inc(par_in, DMA)
            sp.dma_start(a_cols[:, 1:2], a_src.rearrange("(f a) -> f a", a=1)).then_inc(par_in, DMA)
            sp.dma_start(bias_b[:, :], bias.partition_broadcast(P)).then_inc(par_in, DMA)

            def tile(half, hop, first, i, s):
                n, w = n_of(half, first, i, s), w_of(half, first, i, s)
                for q in range(Q):
                    wait_alone(sp, split_ready, n * Q + (q + 1), passed)
                    sp.dma_start(a_raw[:, q, :].rearrange("p (k c) -> p k c", k=KQ),
                                 adj_v[w, :, KQ * q:KQ * (q + 1), :]).then_inc(a_in[q], DMA)
                if first == TURNED:
                    wait_alone(sp, transposed, half * (2 * NT) + (NT + 2), passed)
                    for e in range(2):
                        wait_alone(sp, stage_out[e], half * ((NT + UNTIL) * DMA) + (NT * DMA + DMA), passed)
                sp.wait_ge(summed, n + 1)
                sp.dma_start(ring[:, s, :], z_dram[half, hop, w]).then_inc(zin[s], DMA)

            with sp.Fori(0, 2) as half:
                wait_alone(sp, x1_out, half * (NT * DMA) + DMA, passed)
                wait_alone(sp, transposed, half * (2 * NT) + 2, passed)
                for g in range(4):
                    with sp.Fori(0, 4) as i:
                        sp.dma_start(xh[:, i + 4 * g], x_v[half, i + 4 * g]).then_inc(x_in[g], DMA)
                for hop, first in ((0, TURNED), (0, REST), (1, HOP2)):
                    with sp.Fori(0, UNTIL if hop else UNTIL // 2) as i:
                        for s in range(2):
                            tile(half, hop, first, i, s)

        @block.gpsimd
        def _(pool):
            nc.gpsimd.memset(ident[:, :], 0.0).then_inc(ident_ready, 1)
            pool.wait_ge(ident_ready, 1)
            for k, stores in enumerate((*stage_out, row_out, x1_out, *mask_out)):
                pool.dma_start(pad_dram[k], ident[0:DMA, 0:D]).then_inc(stores, DMA)
            for stores in (*stage_out, row_out, x1_out, *mask_out):
                pool.wait_ge(stores, DMA)
            nc.gpsimd.affine_select(out=ident[:, :], in_=ident[:, :], compare_op=ALU.not_equal, fill=1.0,
                                    base=0, pattern=[[-1, P]], channel_multiplier=1).then_inc(ident_ready, 1)
            with pool.Fori(0, 2) as half:
                with pool.Fori(0, NT) as t:
                    for hop in range(2):
                        pool.wait_ge(z_staged, half * (2 * NT) + t * 2 + (hop + 1))
                        pool.dma_start(z_dram[half, hop, t], stage[:, hop, 0:W]).then_inc(stage_out[hop], DMA)
                with pool.Fori(0, UNTIL) as i:
                    for q in range(Q):
                        pool.wait_ge(mask_copied, half * (UNTIL * Q) + i * Q + (q + 3))
                        pool.dma_start(mt_dram[half * UNTIL + i, :, KQ * P * q:KQ * P * (q + 1)],
                                       mask_t[:, q % 2, :]).then_inc(mask_out[q % 2], DMA)
                with pool.Fori(0, NT) as t:
                    pool.wait_ge(x1_ready, half * NT + t + 1)
                    pool.dma_start(x1_dram[half, t], xh[:, t].rearrange("p b f -> p (b f)")).then_inc(x1_out, DMA)
                with pool.Fori(0, UNTIL) as i:
                    for s in range(2):
                        pool.wait_ge(row_staged, half * NT + i * 2 + (s + 1))
                        pool.dma_start(s_dram[half, i * 2 + s].unsqueeze(0), row_st).then_inc(row_out, DMA)
                        pool.wait_ge(evacuated, v_of(half, 1, i, s) + 3)
                        pool.dma_start(g_dram[half, i * 2 + s], stage[:, s, :]).then_inc(stage_out[s], DMA)
            pool.wait_ge(x1_out, 2 * NT * DMA + DMA)
            pool.wait_ge(row_out, 2 * NT * DMA + DMA)
            for s in range(2):
                pool.wait_ge(stage_out[s], 2 * (NT + UNTIL) * DMA + DMA)
                pool.wait_ge(mask_out[s], 2 * UNTIL * (Q // 2) * DMA + DMA)

        @block.scalar
        def _(act):
            def high(n, turned_base=None):
                for q in range(Q):
                    act.wait_ge(a_in[q], n * DMA + DMA)
                    act.wait_ge(chunk_used, n * Q + (q + 1))
                    nc.scalar.activation(a_hi[:, q].rearrange("p k c -> p (k c)"), a_raw[:, q, :],
                                         ACT.Copy).then_inc(hi_ready, 1)
                    if turned_base is not None:
                        act.wait_ge(mask_turned, turned_base * Q + (q + 3))
                        act.wait_ge(mask_out[q % 2], turned_base * (Q // 2 * DMA) + (q // 2 * DMA + DMA))
                        nc.scalar.activation(mask_t[:, q % 2, :], ps_m[q % 2], ACT.Copy).then_inc(mask_copied, 1)

            def project(half, phase):
                act.wait_ge(norm_ready, half * 2 + (phase + 1))
                with act.Fori(0, UNTIL) as i:
                    for s in range(2):
                        v = v_of(half, phase, i, s)
                        t = i * 2 + s
                        act.wait_ge(transposed, v + 1)
                        for b in range(HB):
                            done = nc.scalar.activation(ring[:, s, D * b:D * (b + 1)], xh[:, t, b, :], ACT.Relu,
                                                        bias=st[:, NMR, bass.ds(t * HB + b, 1)],
                                                        scale=st[:, RSTD, bass.ds(t * HB + b, 1)])
                        done.then_inc(h_ready, 1)
                    for s in range(2):
                        v = v_of(half, phase, i, s)
                        act.wait_ge(transposed, v + 3)
                        act.wait_ge(projected, v + 1)
                        nc.scalar.activation(ring[:, 2 + s, :], ps_t[s], ACT.Copy).then_inc(ht_ready, 1)

            def deviations(half, phase):
                act.wait_ge(var_ready, half * 2 + (phase + 1))
                nc.scalar.activation(st[:, SD, :], st[:, VAR, :], ACT.Sqrt, bias=eps_t[:, :],
                                     scale=1.0 / D).then_inc(sd_ready, 1)

            act.sem_inc(ht_ready, 2)
            act.sem_inc(mask_copied, 2)
            act.wait_ge(set_up, 1)
            with act.Fori(0, 2) as half:
                high(n_of(half, TURNED, 0))
                deviations(half, 0)
                project(half, 0)
                act.wait_ge(row_out, half * (NT * DMA) + DMA)
                with act.Fori(0, UNTIL) as i:
                    high(half * (2 * NT) + i + 1, half * UNTIL + i)
                with act.Fori(0, 2 * NT - 1 - UNTIL) as i:
                    high(half * (2 * NT) + i + (UNTIL + 1))
                deviations(half, 1)
                project(half, 1)

        @block.vector
        def _(dve):
            def low(n, mask_base=None):
                for q in range(Q):
                    dve.wait_ge(hi_ready, n * Q + (q + 1))
                    if mask_base is not None:
                        dve.wait_ge(mask_turned, mask_base + (q + 1))
                        nc.vector.tensor_scalar(mask[:, q % 2, :], a_raw[:, q, :], 0.0, None,
                                                ALU.is_gt).then_inc(mask_ready, 1)
                    nc.vector.tensor_tensor(a_lo[:, q].rearrange("p k c -> p (k c)"), a_raw[:, q, :],
                                            a_hi[:, q].rearrange("p k c -> p (k c)").bitcast(F32),
                                            ALU.subtract).then_inc(split_ready, 1)

            def add_z(half, first, i, s):
                n = n_of(half, first, i, s)
                dve.wait_ge(zin[s], half * (NT * DMA) + i * DMA + (first // 2 + 1) * DMA)
                dve.wait_ge(chunk_used, n * Q + 2 * Q)
                nc.vector.tensor_tensor(ring[:, 2 + s, :], acc[s], ring[:, s, :], ALU.add).then_inc(summed, 1)
                wait_alone(dve, summed, n + 3, passed)

            def end_hop1(half, first, i, s):
                add_z(half, first, i, s)
                m, w = half * NT + i * 2 + (first + s), w_of(half, first, i, s)
                nc.vector.tensor_copy(u_hi[:, w], ring[:, 2 + s, :]).then_inc(uhi_done, 1)
                dve.wait_ge(uhi_done, m + 1)
                nc.vector.tensor_tensor(u_lo[:, w], ring[:, 2 + s, :], u_hi[:, w].bitcast(F32),
                                        ALU.subtract).then_inc(u_ready, 1)

            def row_stats(t):
                for b in range(HB):
                    last = nc.vector.bn_stats(bst[:, bass.ds(t * HB + b, 1), :].rearrange("p a c -> p (a c)"),
                                              xh[:, t, b, :])
                return last

            def end_hop2(half, i, s):
                add_z(half, HOP2, i, s)
                t = i * 2 + s
                xt = xh[:, t].rearrange("p b f -> p (b f)")
                nc.vector.scalar_tensor_tensor(xt, ring[:, 2 + s, :], 0.0, xt, ALU.max, ALU.add).then_inc(x1_ready, 1)
                dve.wait_ge(x1_ready, half * NT + i * 2 + (s + 1))
                row_stats(t).then_inc(stats_done, 1)

            def norms(half, phase):
                c = half * 2 + phase
                dve.wait_ge(stats_done, half * (2 * NT) + (phase + 1) * NT)
                dve.wait_ge(transposed, half * (2 * NT) + (phase * NT + 2))
                nc.vector.tensor_tensor(st[:, MSUM, :], bst[:, :, 1], bst[:, :, 4], ALU.add).then_inc(norm_step, 1)
                nc.vector.tensor_tensor(st[:, DIFF, :], bst[:, :, 1], bst[:, :, 4], ALU.subtract).then_inc(norm_step, 1)
                nc.vector.tensor_tensor(st[:, M2, :], bst[:, :, 2], bst[:, :, 5], ALU.add).then_inc(norm_step, 1)
                dve.wait_ge(norm_step, c * 5 + 3)
                nc.vector.tensor_tensor(st[:, SQ, :], st[:, DIFF, :], st[:, DIFF, :], ALU.mult).then_inc(norm_step, 1)
                dve.wait_ge(norm_step, c * 5 + 4)
                nc.vector.scalar_tensor_tensor(st[:, VAR, :], st[:, SQ, :], D / 4.0, st[:, M2, :],
                                               ALU.mult, ALU.add).then_inc(var_ready, 1)
                dve.wait_ge(sd_ready, c + 1)
                nc.vector.reciprocal(st[:, RSTD, :], st[:, SD, :]).then_inc(norm_step, 1)
                dve.wait_ge(norm_step, c * 5 + 5)
                nc.vector.scalar_tensor_tensor(st[:, NMR, :], st[:, MSUM, :], -0.5, st[:, RSTD, :],
                                               ALU.mult, ALU.mult).then_inc(norm_ready, 1)

            dve.sem_inc(evacuated, 2)
            dve.sem_inc(summed, 2)
            dve.sem_inc(split_ready, Q)
            nc.vector.memset(eps_t[:, :], EPS).then_inc(set_up, 1)
            dve.wait_ge(ident_ready, 2)
            nc.vector.tensor_copy(ident16[:, :], ident[:, :]).then_inc(set_up, 1)
            dve.wait_ge(par_in, 9 * DMA)
            nc.vector.tensor_tensor(t_cat[:, 0, :], th[:, 2, :], th[:, 4, :], ALU.add).then_inc(set_up, 1)
            nc.vector.tensor_tensor(t_cat[:, 1, :], th[:, 1, :], th[:, 3, :], ALU.add).then_inc(set_up, 1)
            dve.wait_ge(set_up, 3)
            nc.vector.tensor_tensor(t_cat[:, 2, :], th[:, 0, :], t_cat[:, 0, :], ALU.subtract).then_inc(set_up, 1)
            dve.wait_ge(set_up, 5)
            nc.vector.tensor_scalar(t_cat[:, 0, :], t_cat[:, 0, :], 2.0, None, ALU.mult).then_inc(set_up, 1)
            dve.wait_ge(w_done, 1)
            nc.vector.tensor_copy(w_t, ps_t[0][:, 0:D]).then_inc(set_up, 1)
            dve.wait_ge(w_done, 2)
            nc.vector.tensor_copy(w_ext[:, D:D + 2], ps_t[1][:, 0:2]).then_inc(set_up, 1)
            with dve.Fori(0, 2) as half:
                for g in range(4):
                    wait_alone(dve, x_in[g], half * (4 * DMA) + 4 * DMA, passed)
                    with dve.Fori(0, 4) as i:
                        row_stats(i + 4 * g).then_inc(stats_done, 1)
                norms(half, 0)
                with dve.Fori(0, UNTIL) as i:
                    for s in range(2):
                        v, t = v_of(half, 0, i, s), i * 2 + s
                        out = half * ((NT + UNTIL) * DMA) + t * DMA + DMA
                        dve.wait_ge(projected, v + 3)
                        nc.vector.tensor_copy(z_hi[:, t], ps_z2[s]).then_inc(zhi_done, 1)
                        z10 = ps_z10[s].rearrange("p u (b c) -> p (u b) c", c=2 * D)
                        to = [stage[:, hop, 0:W].rearrange("p (b f) -> p b f", b=HB) for hop in range(2)]
                        dve.wait_ge(stage_out[0], out)
                        nc.vector.tensor_copy(to[0], z10[:, :, 0:D]).then_inc(z_staged, 1)
                        dve.wait_ge(stage_out[1], out)
                        nc.vector.tensor_tensor(to[1], z10[:, :, D:2 * D],
                                                bias_b[:, :].unsqueeze(1).broadcast_to([P, HB, D]),
                                                ALU.add).then_inc(z_staged, 1)
                        dve.wait_ge(zhi_done, half * NT + t + 1)
                        nc.vector.tensor_tensor(z_lo[:, t], ps_z2[s], z_hi[:, t].bitcast(F32),
                                                ALU.subtract).then_inc(evacuated, 1)
                low(n_of(half, TURNED, 0), half * (UNTIL * Q))
                with dve.Fori(0, UNTIL // 2 - 1) as i:
                    for s in range(2):
                        low(n_of(half, TURNED, i, s) + 1, half * (UNTIL * Q) + i * (2 * Q) + (s + 1) * Q)
                        end_hop1(half, TURNED, i, s)
                low(n_of(half, TURNED, UNTIL // 2 - 1, 1), half * (UNTIL * Q) + (UNTIL - 1) * Q)
                end_hop1(half, TURNED, UNTIL // 2 - 1, 0)
                low(n_of(half, REST, 0))
                end_hop1(half, TURNED, UNTIL // 2 - 1, 1)
                with dve.Fori(0, UNTIL // 2) as i:
                    for s in range(2):
                        low(n_of(half, REST, i, s) + 1)
                        end_hop1(half, REST, i, s)
                with dve.Fori(0, UNTIL - 1) as i:
                    for s in range(2):
                        low(n_of(half, HOP2, i, s) + 1)
                        end_hop2(half, i, s)
                low(n_of(half, HOP2, UNTIL - 1, 1))
                end_hop2(half, UNTIL - 1, 0)
                end_hop2(half, UNTIL - 1, 1)
                norms(half, 1)
                for e in range(2):
                    wait_alone(dve, mask_out[e], half * (UNTIL * Q // 2 * DMA) + (UNTIL * Q // 2 * DMA + DMA), passed)
                with dve.Fori(0, UNTIL) as i:
                    for s in range(2):
                        v, t = v_of(half, 1, i, s), i * 2 + s
                        dve.wait_ge(projected, v + 3)
                        dve.wait_ge(row_out, half * (NT * DMA) + t * DMA + DMA)
                        nc.vector.tensor_copy(row_st, ps_row[s]).then_inc(row_staged, 1)
                        dve.wait_ge(stage_out[s], half * ((NT + UNTIL) * DMA) + i * DMA + (NT * DMA + DMA))
                        nc.vector.tensor_copy(stage[:, s, :].rearrange("p (u c) -> p u c", u=2),
                                              ps_g[s]).then_inc(evacuated, 1)

        @block.tensor
        def _(pe):
            def transposes(v, s):
                pe.wait_ge(h_ready, v + 1)
                pe.wait_ge(ht_ready, v + 1)
                for b in range(HB):
                    last = nc.tensor.transpose(ps_t[s][:, D * b:D * (b + 1)], ring[:, s, D * b:D * (b + 1)], ident[:, :])
                last.then_inc(transposed, 1)

            def tile(half, hop, first, i, s):
                n = n_of(half, first, i, s)
                hi, lo = (u_hi, u_lo) if hop else (z_hi, z_lo)
                pe.wait_ge(summed, n + 1)
                for q in range(Q):
                    pe.wait_ge(split_ready, n * Q + (q + 1 + Q))
                    for kk in range(KQ):
                        k = q * KQ + kk
                        nc.tensor.matmul(acc[s], a_hi[:, q, kk, :], hi[:, k, :], start=k == 0, stop=False)
                        nc.tensor.matmul(acc[s], a_hi[:, q, kk, :], lo[:, k, :], start=False, stop=False)
                        last = nc.tensor.matmul(acc[s], a_lo[:, q, kk, :], hi[:, k, :], start=False, stop=k == NT - 1)
                    last.then_inc(chunk_used, 1)
                    if first == TURNED:
                        c = half * (UNTIL * Q) + i * (2 * Q) + (s * Q + q)
                        pe.wait_ge(mask_ready, c + 1)
                        pe.wait_ge(mask_copied, c + 1)
                        for kk in range(KQ):
                            last = nc.tensor.transpose(ps_m[q % 2][:, P * kk:P * (kk + 1)],
                                                       mask[:, q % 2, P * kk:P * (kk + 1)], ident16[:, :])
                        last.then_inc(mask_turned, 1)

            pe.sem_inc(transposed, 2)
            pe.sem_inc(projected, 2)
            pe.sem_inc(chunk_used, Q)
            pe.sem_inc(mask_turned, 2)
            pe.wait_ge(ident_ready, 2)
            pe.wait_ge(par_in, 9 * DMA)
            nc.tensor.transpose(ps_t[0][:, 0:D], w_ext[:, 0:D], ident[:, :]).then_inc(w_done, 1)
            pe.wait_ge(set_up, 7)
            nc.tensor.matmul(ps_t[1][:, 0:2], w_t, a_cols, start=True, stop=True).then_inc(w_done, 1)
            pe.wait_ge(set_up, 8)
            with pe.Fori(0, 2) as half:
                with pe.Fori(0, UNTIL) as i:
                    for s in range(2):
                        transposes(v_of(half, 0, i, s), s)
                    for s in range(2):
                        v = v_of(half, 0, i, s)
                        pe.wait_ge(ht_ready, v + 3)
                        pe.wait_ge(evacuated, v + 1)
                        for b in range(HB):
                            h_t = ring[:, 2 + s, D * b:D * (b + 1)]
                            nc.tensor.matmul(ps_z2[s][:, D * b:D * (b + 1)], h_t, t_cat[:, 0, :], start=True, stop=True)
                            last = nc.tensor.matmul(ps_z10[s][:, b // 2, 2 * D * (b % 2):2 * D * (b % 2 + 1)], h_t,
                                                    t_cat[:, 1:3, :].rearrange("p a f -> p (a f)"), start=True, stop=True)
                        last.then_inc(projected, 1)
                wait_alone(pe, evacuated, half * (2 * NT) + (NT + 2), passed)
                for first in (TURNED, REST):
                    with pe.Fori(0, UNTIL // 2) as i:
                        for s in range(2):
                            tile(half, 0, first, i, s)
                wait_alone(pe, u_ready, half * NT + NT, passed)
                with pe.Fori(0, UNTIL) as i:
                    for s in range(2):
                        tile(half, 1, HOP2, i, s)
                wait_alone(pe, summed, half * (2 * NT) + (2 * NT + 2), passed)
                with pe.Fori(0, UNTIL) as i:
                    for s in range(2):
                        transposes(v_of(half, 1, i, s), s)
                    for s in range(2):
                        v = v_of(half, 1, i, s)
                        pe.wait_ge(ht_ready, v + 3)
                        pe.wait_ge(evacuated, v + 1)
                        for b in range(HB):
                            nc.tensor.matmul(ps_g[s][:, b // 2, GC * (b % 2):GC * (b % 2 + 1)],
                                             ring[:, 2 + s, D * b:D * (b + 1)], w_ext[:, 0:GC], start=True, stop=True)
                        nc.tensor.matmul(ps_row[s], w_ext[:, GC:GC + 1], ring[:, 2 + s, :],
                                         start=True, stop=True).then_inc(projected, 1)


def layer1(nc, pad_dram, mt_dram, x1_dram, g_dram, s_dram, out):
    ctx = ExitStack()
    with ctx:
        def sb(name, shape, dt=F32):
            return ctx.enter_context(nc.sbuf_tensor(name, shape, dt))

        def sem(name):
            return ctx.enter_context(nc.semaphore(name))

        NW = 4
        PER = 3
        NB = -(-NT // PER)
        mt = sb("mt", [P, NT, N], BF16)
        g = sb("g", [P, 2, NT, GC])
        s_b = sb("s_b", [P, 2, N])
        wt = sb("wt", [P, NW, N])
        x1 = sb("x1", [P, 2, NT, D])
        dm = sb("dm", [P, 2, 5])
        rq = sb("rq", [P, 2, 2, NT])
        pad = sb("pad_zeros", [DMA, D])
        rden = sb("rden", [P, NT])
        ps = ctx.enter_context(nc.psum_tensor("acc", [P, NB, 512], F32))

        passed = sem("passed1")
        mt_in = sem("mt_in")
        g_in = [sem(f"g_in{e}") for e in range(2)]
        s_in = [sem(f"s_in{e}") for e in range(2)]
        x1_in = [sem(f"x1_in{e}") for e in range(2)]
        own_max = sem("own_max")
        all_max = sem("all_max")
        guard = sem("guard")
        factors = sem("factors")
        clipped = sem("clipped")
        t_ready = sem("t_ready")
        g_scaled = sem("g_scaled")
        w_ready = sem("w_ready")
        w_used = sem("w_used")
        bank_done = sem("bank_done")
        batch_out = sem("batch_out")
        bank_free = sem("bank_free")
        inv_done = sem("inv_done")
        stored = [sem(f"stored{e}") for e in range(2)]
        pad_ready = sem("pad_ready")

        mt_v = mt_dram.rearrange("w p n -> p w n")
        g_v = g_dram.rearrange("h t p (b c) -> h b p t c", b=HB)
        s_v = s_dram.rearrange("h t (b c) -> h b t c", b=HB)
        x1_v = x1_dram.rearrange("h t p (b c) -> h b p t c", b=HB)
        out_v = out.rearrange("b (t p) f -> b p t f", p=P)

        block = ctx.enter_context(nc.Block())
        NG = NT // NW

        @block.sync
        def _(sp):
            sp.dma_start(mt[:, 0:NT // 2, :], mt_v[:, 0:NT // 2, :]).then_inc(mt_in, DMA)
            with sp.Fori(0, 2) as half:
                with sp.Fori(0, HB // 2) as i:
                    for e in range(2):
                        b, k = half * HB + i * 2 + e, i * 2 + e
                        sp.wait_ge(bank_free, b * NB + 1)
                        sp.dma_start(g[:, e], g_v[half, k]).then_inc(g_in[e], DMA)
                        sp.dma_start(s_b[:, e, :].rearrange("p (t c) -> p t c", t=NT),
                                     s_v[half, k].partition_broadcast(P)).then_inc(s_in[e], DMA)
                        sp.wait_ge(stored[e], half * (HB // 2 * DMA) + i * DMA + DMA)
                        sp.dma_start(x1[:, e], x1_v[half, k]).then_inc(x1_in[e], DMA)

        @block.gpsimd
        def _(pool):
            def reduce_max(b, e):
                wait_alone(pool, own_max, b + 1, passed)
                nc.gpsimd.partition_all_reduce(dm[:, e, 1:2], dm[:, e, 0:1], P, RMAX).then_inc(all_max, 1)

            def store(b, e):
                pool.wait_ge(bank_free, b * NB + (2 * NB + 1))
                pool.dma_start(out_v[b], x1[:, e]).then_inc(stored[e], DMA)

            nc.gpsimd.memset(pad[:, :], 0.0).then_inc(pad_ready, 1)
            pool.wait_ge(pad_ready, 1)
            for e in range(2):
                pool.dma_start(pad_dram[6 + e], pad[:, :]).then_inc(stored[e], DMA)
            reduce_max(0, 0)
            with pool.Fori(0, B // 2 - 1) as i:
                for e in range(2):
                    reduce_max(i * 2 + (e + 1), 1 - e)
                    store(i * 2 + e, e)
            reduce_max(B - 1, 1)
            store(B - 2, 0)
            store(B - 1, 1)
            for e in range(2):
                pool.wait_ge(stored[e], B // 2 * DMA + DMA)

        @block.scalar
        def _(act):
            act.dma_start(mt[:, NT // 2:NT, :], mt_v[:, NT // 2:NT, :]).then_inc(mt_in, DMA)
            with act.Fori(0, B // 2) as i:
                for e in range(2):
                    b = i * 2 + e
                    act.wait_ge(guard, b * 3 + 3)
                    nc.scalar.activation(rq[:, e, 0, :], g[:, e, :, D], ACT.Exp, bias=dm[:, e, 3:4], scale=1 - SLOPE)
                    nc.scalar.activation(rq[:, e, 1, :], g[:, e, :, D], ACT.Exp, bias=dm[:, e, 4:5], scale=SLOPE)
                    nc.scalar.activation(g[:, e, :, D], g[:, e, :, D], ACT.Exp, bias=dm[:, e, 4:5],
                                         scale=SLOPE).then_inc(factors, 1)
                    act.wait_ge(clipped, b + 1)
                    nc.scalar.activation(s_b[:, e, :], s_b[:, e, :], ACT.Exp, bias=dm[:, e, 3:4],
                                         scale=SLOPE - 1).then_inc(t_ready, 1)

        @block.vector
        def _(dve):
            def own(i, e):
                dve.wait_ge(g_in[e], i * DMA + DMA)
                nc.vector.reduce_max(dm[:, e, 0:1], g[:, e, :, D], AX.X).then_inc(own_max, 1)

            def clip(i, e):
                b = i * 2 + e
                dve.wait_ge(all_max, b + 1)
                for slot, by in ((2, -1.0), (3, SLOPE - 1), (4, -SLOPE)):
                    nc.vector.tensor_scalar(dm[:, e, slot:slot + 1], dm[:, e, 1:2], by, None, ALU.mult).then_inc(guard, 1)
                dve.wait_ge(s_in[e], i * DMA + DMA)
                dve.wait_ge(guard, b * 3 + 3)
                nc.vector.tensor_scalar(s_b[:, e, :], s_b[:, e, :], dm[:, e, 2:3], None, ALU.max).then_inc(clipped, 1)

            def scale(i, e):
                dve.wait_ge(factors, i * 2 + (e + 1))
                nc.vector.tensor_tensor(g[:, e, :, 0:D], g[:, e, :, 0:D],
                                        rq[:, e, 1, :].unsqueeze(2).broadcast_to([P, NT, D]),
                                        ALU.mult).then_inc(g_scaled, 1)

            def weights(i, e, jj, slots):
                b = i * 2 + e
                dve.wait_ge(t_ready, b + 1)
                for u in slots:
                    dve.wait_ge(w_used, b * NT + jj * NW + (u + 1))
                    nc.vector.scalar_tensor_tensor(wt[:, u, :], s_b[:, e, :], rq[:, e, 0, bass.ds(jj * NW + u, 1)],
                                                   mt[:, jj * NW + u, :], ALU.max, ALU.mult).then_inc(w_ready, 1)

            def finish(i, e):
                b = i * 2 + e
                dve.wait_ge(w_used, b * NT + (NT + NW))
                for k in range(NB):
                    n = min(PER, NT - k * PER)
                    nc.vector.reciprocal(rden[:, PER * k:PER * k + n],
                                         ps[:, k, 0:n * GC].rearrange("p (n c) -> p n c", n=n)[:, :, D]).then_inc(inv_done, 1)
                dve.wait_ge(x1_in[e], i * DMA + DMA)
                dve.wait_ge(inv_done, b * NB + NB)
                for t in range(NT):
                    last = nc.vector.scalar_tensor_tensor(x1[:, e, t, :], ps[:, t // PER, GC * (t % PER):GC * (t % PER) + D],
                                                          rden[:, t:t + 1], x1[:, e, t, :], ALU.mult, ALU.add)
                    if t % PER == PER - 1 or t == NT - 1:
                        last.then_inc(bank_free, 1)

            def batch(i, e, last=False):
                nxt = (i, 1) if e == 0 else (i + 1, 0)
                weights(i, e, 0, range(NW - 1, NW))
                weights(i, e, 1, range(NW))
                if not last:
                    own(*nxt)
                weights(i, e, 2, range(NW))
                if not last:
                    clip(*nxt)
                weights(i, e, NG - 1, range(NW))
                if not last:
                    scale(*nxt)
                    weights(*nxt, 0, range(NW - 1))
                finish(i, e)

            dve.sem_inc(bank_free, NB + 1)
            own(0, 0)
            clip(0, 0)
            scale(0, 0)
            dve.wait_ge(mt_in, 2 * DMA)
            weights(0, 0, 0, range(NW - 1))
            with dve.Fori(0, B // 2 - 1) as i:
                for e in range(2):
                    batch(i, e)
            batch(B // 2 - 1, 0)
            batch(B // 2 - 1, 1, last=True)

        @block.tensor
        def _(pe):
            def group(b, e, jj, first):
                for u in range(NW):
                    pe.wait_ge(w_ready, b * NT + jj * NW + (u + 1))
                    for t in range(NT):
                        opens = first and u == 0 and t % PER == 0
                        if opens:
                            pe.wait_ge(bank_free, b * NB + (t // PER + 2))
                        col = GC * (t % PER)
                        last = nc.tensor.matmul(ps[:, t // PER, col:col + GC], wt[:, u, P * t:P * (t + 1)],
                                                g[:, e, jj * NW + u, :], start=opens, stop=True, skip_group_check=True)
                    last.then_inc(w_used, 1)

            pe.sem_inc(w_used, NW)
            with pe.Fori(0, B // 2) as i:
                for e in range(2):
                    b = i * 2 + e
                    pe.wait_ge(g_scaled, b + 1)
                    group(b, e, 0, True)
                    with pe.Fori(1, NG) as jj:
                        group(b, e, jj, False)


def build(nc, x, adj, theta, bias, gw, a_src, a_dst, out):
    pad_dram = nc.dram_tensor("pad", (8, DMA, D), F32).ap()
    z_dram = nc.dram_tensor("z_scratch", (2, 2, NT, P, W), F32).ap()
    mt_dram = nc.dram_tensor("mask_scratch", (NT, P, N), BF16).ap()
    x1_dram = nc.dram_tensor("x1_scratch", (2, NT, P, W), F32).ap()
    g_dram = nc.dram_tensor("g_scratch", (2, NT, P, HB * GC), F32).ap()
    s_dram = nc.dram_tensor("s_scratch", (2, NT, W), F32).ap()
    layer0(nc, pad_dram, x, adj, theta, bias, gw, a_src, a_dst, z_dram, mt_dram, x1_dram, g_dram, s_dram)
    layer1(nc, pad_dram, mt_dram, x1_dram, g_dram, s_dram, out)


INPUTS = ["x", "adj", "L0_gnn_Theta1", "L0_gnn_bias", "L1_gnn_w", "L1_gnn_a_src", "L1_gnn_a_dst"]


def kernel(**inputs):
    import numpy as np
    import concourse.bacc as bacc
    from concourse.bass_utils import run_bass_kernel_spmd

    nc = bacc.Bacc("TRN2", target_bir_lowering=False, num_devices=1)
    arrays = {f"in_{n}": np.ascontiguousarray(inputs[n]) for n in INPUTS}
    aps = [nc.dram_tensor(n, a.shape, mybir.dt.from_np(a.dtype), kind="ExternalInput").ap() for n, a in arrays.items()]
    out = nc.dram_tensor("out", (B, N, D), F32, kind="ExternalOutput").ap()
    build(nc, *aps, out)
    return run_bass_kernel_spmd(nc, [arrays], core_ids=[0]).results[0]["out"]
```

```python
import concourse.bass as bass
from concourse import mybir
from contextlib import ExitStack

F32 = mybir.dt.float32
F32R = mybir.dt.float32r
BF16 = mybir.dt.bfloat16
ALU = mybir.AluOpType
ACT = mybir.ActivationFunctionType
AX = mybir.AxisListType
RMAX = bass.bass_isa.ReduceOp.max

P = 128
B, N, D = 8, 2048, 128
HB = B // 2
W = HB * D
NT = N // P
Q = 4
KQ = NT // Q
EPS = 1e-5
SLOPE = 0.2
GC = D + 1
GE = D + 2
GB = HB - 1
DMA = 16


def wait_alone(eng, sem, value, passed):
    eng.wait_ge(sem, value)
    eng.sem_inc(passed, 1)


def wait(eng, sem, value):
    if not isinstance(value, int) or value > 0:
        eng.wait_ge(sem, value)


def mask_view(zm):
    return zm.rearrange("p a t w -> p (a t w)").bitcast(BF16).rearrange("p (k n) -> p k n", k=NT)


def layer0(nc, zm, x, adj, theta, bias, gw, a_src, a_dst, z_dram, mt_dram, x1_dram, g_dram, s_dram):
    ctx = ExitStack()
    with ctx:
        def sb(name, shape, dt=F32):
            return ctx.enter_context(nc.sbuf_tensor(name, shape, dt))

        def sem(name):
            return ctx.enter_context(nc.semaphore(name))

        z_hi, z_lo, mt = zm[:, 0], zm[:, 1], mask_view(zm)
        u_hi = sb("u_hi", [P, NT, W], F32R)
        u_lo = sb("u_lo", [P, NT, W], F32R)
        a_raw = sb("a_raw", [P, Q, KQ * P])
        a_hi = sb("a_hi", [P, Q, KQ, P], F32R)
        a_lo = sb("a_lo", [P, Q, KQ, P], F32R)
        xt = sb("xt", [P, 4, HB, D])
        h = sb("h", [P, 2, W])
        ht = sb("ht", [P, 2, W])
        zin = sb("zin", [P, 2, W])
        total = sb("total", [P, 2, W])
        z_st = sb("z_st", [P, 2, 2, W])
        g_st = sb("g_st", [P, HB, GE])
        s_keep = sb("s_keep", [P, HB, NT])
        s_row = sb("s_row", [HB * NT, P])
        mask = sb("mask", [P, Q, KQ * P], BF16)
        mask_t = sb("mask_t", [P, 2, KQ * P], BF16)
        ident = sb("ident", [P, P])
        ident16 = sb("ident16", [P, P], BF16)
        t_cat = sb("t_cat", [P, 3, D])
        bias_b = sb("bias_b", [P, D])
        w_ext = sb("w_ext", [P, D + 2])
        bst = sb("bst", [P, 2, HB, 6])
        mv = sb("mv", [P, 2, HB, 2])
        sd = sb("sd", [P, 2, HB])
        rstd = sb("rstd", [P, 2, HB])
        nmr = sb("nmr", [P, 2, HB])
        eps_t = sb("eps_t", [P, 1])
        ps = ctx.enter_context(nc.psum_tensor("ps", [P, 8, 512], F32))
        acc = [ps[:, s, :] for s in range(2)]
        PS_T = (2, 1)
        PS_Z2 = (3, 0)
        PS_Z1 = (4, 6)
        PS_Z0 = (5, 7)
        PS_G = (6, 7)
        ps_m = [ps[:, 6 + e, 0:KQ * P // 2].bitcast(BF16) for e in range(2)]
        th = z_st[:, 0].rearrange("p a w -> p (a w)")[:, 0:5 * D].rearrange("p (m d) -> p m d", m=5)
        w_t = g_st[:, 0, 0:D]
        a_cols = g_st[:, 0, D:D + 2]

        par_in = sem("par_in")
        ident_ready = sem("ident_ready")
        set_up = sem("set_up")
        w_done = sem("w_done")
        passed = sem("passed")
        x_in = [sem(f"x_in{k}") for k in range(4)]
        bn_done = sem("bn_done")
        var_ready = sem("var_ready")
        sd_ready = sem("sd_ready")
        rstd_done = sem("rstd_done")
        norm_ready = sem("norm_ready")
        h_ready = sem("h_ready")
        transposed = sem("transposed")
        ht_ready = sem("ht_ready")
        projected = sem("projected")
        evacuated = sem("evacuated")
        zhi_done = sem("zhi_done")
        z1_staged = sem("z1_staged")
        z0_staged = sem("z0_staged")
        z_out = [[sem(f"z_out{hop}{e}") for e in range(2)] for hop in range(2)]
        s_turned = sem("s_turned")
        s_staged = sem("s_staged")
        s_out = sem("s_out")
        mt_in = sem("mt_in")
        g_out = sem("g_out")
        a_in = [sem(f"a_in{q}") for q in range(Q)]
        hi_ready = sem("hi_ready")
        split_ready = sem("split_ready")
        chunk_used = sem("chunk_used")
        z_in = [sem(f"z_in{s}") for s in range(2)]
        summed = sem("summed")
        uhi_done = sem("uhi_done")
        u_ready = sem("u_ready")
        x1_ready = sem("x1_ready")
        x1_out = [sem(f"x1_out{s}") for s in range(2)]
        mask_ready = sem("mask_ready")
        mask_turned = sem("mask_turned")
        mask_copied = sem("mask_copied")
        mask_out = [sem(f"mask_out{e}") for e in range(2)]

        x_v = x.rearrange("(h b) (t p) f -> h t p b f", b=HB, p=P)
        adj_v = adj.rearrange("(k p) (w c) -> w p k c", p=P, c=P)

        def tile_no(half, hop, w):
            return (2 * half + hop) * NT + w

        def job_a(half, t):
            return t * 2 + NT if half else t

        def job_c(half, t):
            return t + 3 * NT if half else t * 2 + (NT + 1)

        def pairs(eng, body, first=0, last=NT // 2):
            with eng.Fori(first, last) as i:
                for s in range(2):
                    body(i, s)

        def quads(eng, step, between=None):
            for u in range(4):
                step(0, u)
            if between:
                between()
            with eng.Fori(1, NT // 4 - 1) as i:
                for u in range(4):
                    step(i, u)
            for u in range(4):
                step(NT // 4 - 1, u)

        def is_last(t, more):
            return isinstance(t, int) and t + more >= NT

        block = ctx.enter_context(nc.Block())

        @block.sync
        def _(sp):
            for m in range(5):
                sp.dma_start(th[:, m, :], theta[m * D:(m + 1) * D, :]).then_inc(par_in, DMA)
            sp.dma_start(w_ext[:, 0:D], gw).then_inc(par_in, DMA)
            sp.dma_start(a_cols[:, 0:1], a_dst.rearrange("(f a) -> f a", a=1)).then_inc(par_in, DMA)
            sp.dma_start(a_cols[:, 1:2], a_src.rearrange("(f a) -> f a", a=1)).then_inc(par_in, DMA)
            sp.dma_start(bias_b[:, :], bias.partition_broadcast(P)).then_inc(par_in, DMA)

            def chunks(n, w):
                for q in range(Q):
                    wait_alone(sp, split_ready, n * Q + (q + 1), passed)
                    sp.dma_start(a_raw[:, q, :].rearrange("p (k c) -> p k c", k=KQ),
                                 adj_v[w, :, KQ * q:KQ * (q + 1), :]).then_inc(a_in[q], DMA)

            def x_tile(half, t, slot, free_at):
                wait_alone(sp, h_ready, free_at, passed)
                sp.dma_start(xt[:, slot], x_v[half, t]).then_inc(x_in[slot], DMA)

            def z_tile(half, hop, w, s):
                wait_alone(sp, summed, tile_no(half, hop, w) + 1, passed)
                sp.dma_start(zin[:, s, :], z_dram[half, hop, w]).then_inc(z_in[s], DMA)

            for t in range(4):
                sp.dma_start(xt[:, t], x_v[0, t]).then_inc(x_in[t], DMA)
            chunks(0, 0)
            with sp.Fori(1, NT // 4) as i:
                for u in range(4):
                    wait_alone(sp, h_ready, i * 4 + (u - 1), passed)
                    sp.dma_start(xt[:, u], x_v[0, i * 4 + u]).then_inc(x_in[u], DMA)
            for half in range(2):
                def hop1(i, s):
                    w = i * 2 + s
                    if not is_last(w, 1):
                        chunks(tile_no(half, 0, w) + 1, w + 1)
                    else:
                        chunks(tile_no(half, 1, 0), 0)
                    z_tile(half, 0, w, s)

                def hop2(i, s):
                    w = i * 2 + s
                    if half == 0:
                        if isinstance(i, int) and i == 0:
                            sp.wait_ge(h_ready, NT + 2)
                        else:
                            wait_alone(sp, h_ready, i * 4 + (2 * s + NT - 1), passed)
                        sp.dma_start(xt[:, s], x_v[1, w]).then_inc(x_in[s], DMA)
                    if not is_last(w, 1):
                        chunks(tile_no(half, 1, w) + 1, w + 1)
                    elif half == 0:
                        chunks(tile_no(1, 0, 0), 0)
                    z_tile(half, 1, w, s)
                    if isinstance(i, int) and i == 0:
                        sp.wait_ge(h_ready, job_c(0, NT - 2 + s) + 3 if half else NT + 2)
                        wait(sp, x1_out[s], half * (NT // 2 * DMA))
                    else:
                        wait_alone(sp, h_ready, i * 2 + (3 * NT + s + 1) if half else i * 4 + (NT + 2 * s), passed)
                        wait_alone(sp, x1_out[s], i * DMA + half * (NT // 2 * DMA), passed)
                    sp.dma_start(xt[:, 2 + s], x_v[half, w]).then_inc(x_in[2 + s], DMA)
                    if half == 1:
                        sp.dma_start(mt[:, w, :], mt_dram[w]).then_inc(mt_in, DMA)

                for stored in z_out[0] + z_out[1]:
                    sp.wait_ge(stored, (half + 1) * (NT // 2 * DMA))
                pairs(sp, hop1, 0, NT // 2 - 1)
                for s in range(2):
                    hop1(NT // 2 - 1, s)
                if half == 1:
                    sp.wait_ge(chunk_used, (tile_no(1, 0, NT - 1) + 2) * Q)
                    for stored in mask_out:
                        sp.wait_ge(stored, NT * Q // 2 * DMA)
                for s in range(2):
                    hop2(0, s)
                pairs(sp, hop2, 1, NT // 2 - 1)
                for s in range(2):
                    hop2(NT // 2 - 1, s)

        @block.gpsimd
        def _(pool):
            nc.gpsimd.memset(ident[:, :], 0.0).then_inc(ident_ready, 1)
            pool.wait_ge(ident_ready, 1)
            nc.gpsimd.affine_select(out=ident[:, :], in_=ident[:, :], compare_op=ALU.not_equal, fill=1.0,
                                    base=0, pattern=[[-1, P]], channel_multiplier=1).then_inc(ident_ready, 1)

            def store_z(half, t, e):
                pool.wait_ge(z1_staged, t + (half * NT + 3))
                pool.dma_start(z_dram[half, 0, t], z_st[:, 0, e, :]).then_inc(z_out[0][e], DMA)
                pool.wait_ge(z0_staged, t + (half * NT + 1))
                pool.dma_start(z_dram[half, 1, t], z_st[:, 1, e, :]).then_inc(z_out[1][e], DMA)

            def store_c(half, t):
                pool.wait_ge(evacuated, job_c(half, t) + 3)
                pool.dma_start(g_dram[half, t], g_st[:, :, :].rearrange("p b c -> p (b c)")).then_inc(g_out, DMA)

            with pool.Fori(0, NT // 2) as i:
                for e in range(2):
                    store_z(0, i * 2 + e, e)
            with pool.Fori(0, NT) as w:
                for q in range(Q):
                    pool.wait_ge(mask_copied, w * Q + (q + 3))
                    pool.dma_start(mt_dram[w, :, KQ * P * q:KQ * P * (q + 1)],
                                   mask_t[:, q % 2, :]).then_inc(mask_out[q % 2], DMA)
            for half in range(2):
                def hop2(i, s):
                    w = i * 2 + s
                    if not isinstance(i, int) or w >= 2:
                        store_c(half, w - 2)
                    if half == 0 and (not isinstance(i, int) or w >= 1):
                        store_z(1, w - 1, 1 - s)
                    pool.wait_ge(x1_ready, w + (half * NT + 1))
                    pool.dma_start(x1_dram[half, w], xt[:, 2 + s].rearrange("p b f -> p (b f)")).then_inc(x1_out[s], DMA)

                for s in range(2):
                    hop2(0, s)
                pairs(pool, hop2, 1)
                store_c(half, NT - 2)
                if half == 0:
                    store_z(1, NT - 1, 1)
                store_c(half, NT - 1)
                pool.wait_ge(s_staged, half + 1)
                pool.dma_start(s_dram[half], s_row[:, :]).then_inc(s_out, DMA)
            for out_sem, n in [(s_out, 2), (g_out, 2 * NT), (mt_in, NT)] + [(m, NT) for m in x1_out]:
                pool.wait_ge(out_sem, n * DMA)

        @block.scalar
        def _(act):
            def high(n, q):
                act.wait_ge(a_in[q], n * DMA + DMA)
                act.wait_ge(chunk_used, n * Q + (q + 1))
                nc.scalar.activation(a_hi[:, q].rearrange("p k c -> p (k c)"), a_raw[:, q, :],
                                     ACT.Copy).then_inc(hi_ready, 1)

            def turned(w, q):
                act.wait_ge(mask_turned, w * Q + (q + 1 + Q))
                wait(act, mask_out[q % 2], w * (Q // 2 * DMA) + q // 2 * DMA)
                nc.scalar.activation(mask_t[:, q % 2, :], ps_m[q % 2], ACT.Copy).then_inc(mask_copied, 1)

            def deviation(v, s):
                act.wait_ge(var_ready, v + 1)
                nc.scalar.activation(sd[:, s, :], mv[:, s, :, 1], ACT.Sqrt, bias=eps_t[:, :]).then_inc(sd_ready, 1)

            def normalise(v, s, slot):
                act.wait_ge(norm_ready, v + 1)
                act.wait_ge(transposed, v + 1)
                for b in range(HB):
                    done = nc.scalar.activation(h[:, s, D * b:D * (b + 1)], xt[:, slot, b, :], ACT.Relu,
                                                bias=nmr[:, s, b:b + 1], scale=rstd[:, s, b:b + 1])
                done.then_inc(h_ready, 1)

            def copy_ht(v, s, bank):
                act.wait_ge(transposed, v + 3)
                act.wait_ge(projected, v + 1)
                nc.scalar.activation(ht[:, s, :], ps[:, bank, :], ACT.Copy).then_inc(ht_ready, 1)

            def stage_z1(v, k, e, stored):
                act.wait_ge(projected, v + 3)
                wait(act, z_out[0][e], stored * DMA)
                nc.scalar.activation(z_st[:, 0, e, :], ps[:, PS_Z1[k], :], ACT.Copy).then_inc(z1_staged, 1)

            for ring in (h_ready, ht_ready, z1_staged, mask_copied):
                act.sem_inc(ring, 2)
            act.wait_ge(set_up, 1)

            deviation(0, 0)
            normalise(0, 0, 0)
            deviation(1, 1)
            copy_ht(0, 0, PS_T[0])

            def step(i, u):
                t = i * 4 + u
                if not is_last(t, 1):
                    normalise(t + 1, (u + 1) % 2, (u + 1) % 4)
                if not is_last(t, 2):
                    deviation(t + 2, u % 2)
                if not is_last(t, 1):
                    copy_ht(t + 1, (u + 1) % 2, PS_T[(u + 1) % 2])
                if not isinstance(t, int) or t >= 1:
                    stage_z1(t - 1, (u + 1) % 2, (u + 1) % 2, i * 2 + (u - 1) // 2)

            quads(act, step, lambda: [high(0, q) for q in range(Q)])
            stage_z1(NT - 1, 1, 1, NT // 2 - 1)

            for half in range(2):
                def hop1(w):
                    for q in range(Q):
                        high(tile_no(half, 0, w) + 1, q)
                        if half == 0:
                            turned(w, q)

                hop1(0)
                with act.Fori(1, NT) as w:
                    hop1(w)

                def hop2(i, s):
                    w = i * 2 + s
                    later = not isinstance(i, int) or w >= 1
                    last = half == 1 and is_last(w, 1)
                    sc, sa = ((1 - s) % 2 if half else 1), 0
                    if not last:
                        high(tile_no(half, 1, w) + 1, 0)
                    if later:
                        deviation(job_c(half, w - 1), sc)
                        normalise(job_c(half, w - 1), sc, 2 + (1 - s))
                    if not last:
                        high(tile_no(half, 1, w) + 1, 1)
                    if half == 0:
                        if later:
                            stage_z1(job_a(1, w - 1), 0, 1 - s, i + (NT // 2 + s - 1))
                        deviation(job_a(1, w), sa)
                        normalise(job_a(1, w), sa, s)
                    if not last:
                        high(tile_no(half, 1, w) + 1, 2)
                    if later:
                        copy_ht(job_c(half, w - 1), sc, PS_T[0])
                    if not last:
                        high(tile_no(half, 1, w) + 1, 3)
                    if half == 0:
                        copy_ht(job_a(1, w), sa, PS_T[0])

                for s in range(2):
                    hop2(0, s)
                pairs(act, hop2, 1, NT // 2 - 1)
                for s in range(2):
                    hop2(NT // 2 - 1, s)
                v = job_c(half, NT - 1)
                deviation(v, v % 2)
                normalise(v, v % 2, 3)
                if half == 0:
                    stage_z1(job_a(1, NT - 1), 0, 1, NT - 1)
                copy_ht(v, v % 2, PS_T[0])

        @block.vector
        def _(dve):
            def low(n, q, w=None):
                dve.wait_ge(hi_ready, n * Q + (q + 1))
                if w is not None:
                    dve.wait_ge(mask_turned, w * Q + (q + 1))
                    nc.vector.tensor_scalar(mask[:, q, :], a_raw[:, q, :], 0.0, None, ALU.is_gt).then_inc(mask_ready, 1)
                nc.vector.tensor_tensor(a_lo[:, q].rearrange("p k c -> p (k c)"), a_raw[:, q, :],
                                        a_hi[:, q].rearrange("p k c -> p (k c)").bitcast(F32),
                                        ALU.subtract).then_inc(split_ready, 1)

            def add_z(half, hop, i, s):
                n = tile_no(half, hop, i * 2 + s)
                dve.wait_ge(z_in[s], i * DMA + ((2 * half + hop) * (NT // 2) + 1) * DMA)
                dve.wait_ge(chunk_used, n * Q + 2 * Q)
                nc.vector.tensor_tensor(total[:, s, :], acc[s], zin[:, s, :], ALU.add).then_inc(summed, 1)
                wait_alone(dve, summed, n + 3, passed)

            def end_hop1(half, i, s):
                add_z(half, 0, i, s)
                w = i * 2 + s
                nc.vector.tensor_copy(u_hi[:, w], total[:, s, :]).then_inc(uhi_done, 1)
                dve.wait_ge(uhi_done, w + (half * NT + 1))
                nc.vector.tensor_tensor(u_lo[:, w], total[:, s, :], u_hi[:, w].bitcast(F32),
                                        ALU.subtract).then_inc(u_ready, 1)

            def stats(v, s, slot):
                dve.wait_ge(h_ready, v + 1)
                for b in range(HB):
                    last = nc.vector.bn_stats(bst[:, s, b, :], xt[:, slot, b, :])
                last.then_inc(bn_done, 1)
                wait_alone(dve, bn_done, v + 1, passed)
                for b in range(HB):
                    last = nc.vector.bn_aggr(mv[:, s, b, :], bst[:, s, b, :])
                last.then_inc(var_ready, 1)

            def norms(v, s):
                dve.wait_ge(sd_ready, v + 1)
                nc.vector.reciprocal(rstd[:, s, :], sd[:, s, :]).then_inc(rstd_done, 1)
                dve.wait_ge(rstd_done, v + 1)
                nc.vector.scalar_tensor_tensor(nmr[:, s, :], mv[:, s, :, 0], -1.0, rstd[:, s, :],
                                               ALU.mult, ALU.mult).then_inc(norm_ready, 1)

            def evacuate_a(v, a, t, k, e, stored):
                dve.wait_ge(projected, v + 3)
                wait(dve, z_out[1][e], stored * DMA)
                z0 = ps[:, PS_Z0[k], :].rearrange("p (b f) -> p b f", b=HB)
                nc.vector.tensor_tensor(z_st[:, 1, e, :].rearrange("p (b f) -> p b f", b=HB), z0,
                                        bias_b[:, :].unsqueeze(1).broadcast_to([P, HB, D]), ALU.add).then_inc(z0_staged, 1)
                nc.vector.tensor_copy(z_hi[:, t], ps[:, PS_Z2[k], :]).then_inc(zhi_done, 1)
                dve.wait_ge(zhi_done, a + 1)
                nc.vector.tensor_tensor(z_lo[:, t], ps[:, PS_Z2[k], :], z_hi[:, t].bitcast(F32),
                                        ALU.subtract).then_inc(evacuated, 1)

            def evacuate_c(half, t):
                dve.wait_ge(projected, job_c(half, t) + 3)
                wait(dve, g_out, t * DMA + half * (NT * DMA))
                nc.vector.tensor_copy(g_st[:, 0:GB, :].rearrange("p b c -> p (b c)"), ps[:, PS_G[0], 0:GB * GE])
                nc.vector.tensor_copy(g_st[:, GB, :], ps[:, PS_G[1], 0:GE])
                wait(dve, s_turned, half)
                nc.vector.tensor_copy(s_keep[:, 0:GB, t], ps[:, PS_G[0], 0:GB * GE].rearrange("p (b c) -> p b c", c=GE)[:, :, D + 1])
                nc.vector.tensor_copy(s_keep[:, GB:HB, t], ps[:, PS_G[1], D + 1:GE]).then_inc(evacuated, 1)

            dve.sem_inc(evacuated, 2)
            dve.sem_inc(summed, 2)
            dve.sem_inc(split_ready, Q)
            nc.vector.memset(eps_t[:, :], EPS).then_inc(set_up, 1)
            dve.wait_ge(ident_ready, 2)
            nc.vector.tensor_copy(ident16[:, :], ident[:, :]).then_inc(set_up, 1)
            dve.wait_ge(par_in, 9 * DMA)
            nc.vector.tensor_tensor(t_cat[:, 0, :], th[:, 2, :], th[:, 4, :], ALU.add).then_inc(set_up, 1)
            nc.vector.tensor_tensor(t_cat[:, 1, :], th[:, 1, :], th[:, 3, :], ALU.add).then_inc(set_up, 1)
            dve.wait_ge(set_up, 3)
            nc.vector.tensor_tensor(t_cat[:, 2, :], th[:, 0, :], t_cat[:, 0, :], ALU.subtract).then_inc(set_up, 1)
            dve.wait_ge(set_up, 5)
            nc.vector.tensor_scalar(t_cat[:, 0, :], t_cat[:, 0, :], 2.0, None, ALU.mult).then_inc(set_up, 1)
            dve.wait_ge(w_done, 1)
            nc.vector.tensor_copy(w_t, ps[:, PS_T[0], 0:D]).then_inc(set_up, 1)
            dve.wait_ge(w_done, 2)
            nc.vector.tensor_copy(w_ext[:, D:D + 2], ps[:, PS_T[1], 0:2]).then_inc(set_up, 1)

            def ahead(i, u):
                t = i * 4 + u
                dve.wait_ge(x_in[u % 4], i * DMA + (u // 4 + 1) * DMA)
                stats(t, u % 2, u % 4)
                norms(t, u % 2)

            def step(i, u):
                t = i * 4 + u
                if not is_last(t, 2):
                    ahead(i, u + 2)
                evacuate_a(t, t, t, u % 2, u % 2, i * 2 + u // 2)

            ahead(0, 0)
            ahead(0, 1)
            quads(dve, step, lambda: [low(0, q, 0) for q in range(Q)])

            for half in range(2):
                def hop1(i, s):
                    w = i * 2 + s
                    for q in range(Q):
                        low(tile_no(half, 0, w) + 1, q, w + 1 if half == 0 and not is_last(w, 1) else None)
                    end_hop1(half, i, s)

                pairs(dve, hop1, 0, NT // 2 - 1)
                for s in range(2):
                    hop1(NT // 2 - 1, s)

                def hop2(i, s):
                    w = i * 2 + s
                    later, second = (not isinstance(i, int) or w >= k for k in (1, 2))
                    last = half == 1 and is_last(w, 1)
                    sc, sa = ((1 - s) if half else 1), 0
                    if not last:
                        low(tile_no(half, 1, w) + 1, 0)
                    if later:
                        norms(job_c(half, w - 1), sc)
                    if half == 0:
                        dve.wait_ge(x_in[s], i * DMA + (NT // 4 + 1) * DMA)
                        stats(job_a(1, w), sa, s)
                    if second:
                        evacuate_c(half, w - 2)
                    if not last:
                        low(tile_no(half, 1, w) + 1, 1)
                    if half == 0:
                        if later:
                            evacuate_a(job_a(1, w - 1), w + (NT - 1), w - 1, 0, 1 - s, i + (NT // 2 + s - 1))
                        norms(job_a(1, w), sa)
                    if not last:
                        low(tile_no(half, 1, w) + 1, 2)
                        low(tile_no(half, 1, w) + 1, 3)
                    add_z(half, 1, i, s)
                    dve.wait_ge(x_in[2 + s], i * DMA + (NT // 4 + half * (NT // 2) + 1) * DMA)
                    xs = xt[:, 2 + s].rearrange("p b f -> p (b f)")
                    nc.vector.scalar_tensor_tensor(xs, total[:, s, :], 0.0, xs, ALU.max, ALU.add).then_inc(x1_ready, 1)
                    dve.wait_ge(x1_ready, w + (half * NT + 1))
                    stats(job_c(half, w), s if half else 1, 2 + s)

                for i in range(2):
                    for s in range(2):
                        hop2(i, s)
                pairs(dve, hop2, 2, NT // 2 - 1)
                for s in range(2):
                    hop2(NT // 2 - 1, s)
                norms(job_c(half, NT - 1), 1)
                evacuate_c(half, NT - 2)
                if half == 0:
                    evacuate_a(job_a(1, NT - 1), 2 * NT - 1, NT - 1, 0, 1, NT - 1)
                evacuate_c(half, NT - 1)
                dve.wait_ge(s_turned, half + 1)
                wait(dve, s_out, half * DMA)
                nc.vector.tensor_copy(s_row[:, :], ps[0:HB * NT, PS_T[0], 0:P]).then_inc(s_staged, 1)

        @block.tensor
        def _(pe):
            def transposes(v, s, bank, shared=False):
                pe.wait_ge(h_ready, v + 3)
                pe.wait_ge(ht_ready, v + 1 + shared)
                for b in range(HB):
                    last = nc.tensor.transpose(ps[:, bank, D * b:D * (b + 1)], h[:, s, D * b:D * (b + 1)], ident[:, :])
                last.then_inc(transposed, 1)

            def project_a(v, a, s, k, shared=False):
                pe.wait_ge(ht_ready, v + 3)
                pe.wait_ge(evacuated, v + 1)
                pe.wait_ge(z1_staged, a + 1 + shared)
                for b in range(HB):
                    h_t = ht[:, s, D * b:D * (b + 1)]
                    for m, bank in enumerate((PS_Z2[k], PS_Z1[k], PS_Z0[k])):
                        last = nc.tensor.matmul(ps[:, bank, D * b:D * (b + 1)], h_t, t_cat[:, m, :], start=True, stop=True)
                last.then_inc(projected, 1)

            def project_c(v, s, shared):
                pe.wait_ge(ht_ready, v + 3)
                pe.wait_ge(evacuated, v + 1 + shared)
                for b in range(HB):
                    col = GE * (b % GB)
                    last = nc.tensor.matmul(ps[:, PS_G[b // GB], col:col + GE], ht[:, s, D * b:D * (b + 1)], w_ext[:, :],
                                            start=True, stop=True)
                last.then_inc(projected, 1)

            def chunk(half, hop, w, s, q):
                n = tile_no(half, hop, w)
                hi, lo = (u_hi, u_lo) if hop else (z_hi, z_lo)
                if q == 0:
                    pe.wait_ge(summed, n + 1)
                pe.wait_ge(split_ready, n * Q + (q + 1 + Q))
                for kk in range(KQ):
                    k = q * KQ + kk
                    nc.tensor.matmul(acc[s], a_hi[:, q, kk, :], hi[:, k, :], start=k == 0, stop=False)
                    nc.tensor.matmul(acc[s], a_hi[:, q, kk, :], lo[:, k, :], start=False, stop=False)
                    last = nc.tensor.matmul(acc[s], a_lo[:, q, kk, :], hi[:, k, :], start=False, stop=k == NT - 1)
                last.then_inc(chunk_used, 1)

            pe.sem_inc(transposed, 2)
            pe.sem_inc(projected, 2)
            pe.sem_inc(chunk_used, Q)
            pe.sem_inc(mask_turned, Q)
            pe.wait_ge(ident_ready, 2)
            pe.wait_ge(par_in, 9 * DMA)
            nc.tensor.transpose(ps[:, PS_T[0], 0:D], w_ext[:, 0:D], ident[:, :]).then_inc(w_done, 1)
            pe.wait_ge(set_up, 7)
            nc.tensor.matmul(ps[:, PS_T[1], 0:2], w_t, a_cols, start=True, stop=True).then_inc(w_done, 1)
            pe.wait_ge(set_up, 8)

            def step(i, u):
                t = i * 4 + u
                if not is_last(t, 1):
                    transposes(t + 1, (u + 1) % 2, PS_T[(u + 1) % 2])
                project_a(t, t, u % 2, u % 2)

            transposes(0, 0, PS_T[0])
            quads(pe, step)
            for half in range(2):
                pe.wait_ge(evacuated, job_a(half, NT - 1) + 3)
                pe.wait_ge(z1_staged, (half + 1) * NT + 2)

                def hop1(i, s):
                    w = i * 2 + s
                    for q in range(Q):
                        chunk(half, 0, w, s, q)
                        if half == 0:
                            pe.wait_ge(mask_ready, w * Q + (q + 1))
                            pe.wait_ge(mask_copied, w * Q + (q + 1))
                            for kk in range(KQ):
                                last = nc.tensor.transpose(ps_m[q % 2][:, P * kk:P * (kk + 1)],
                                                           mask[:, q, P * kk:P * (kk + 1)], ident16[:, :])
                            last.then_inc(mask_turned, 1)

                pairs(pe, hop1)

                def hop2(i, s):
                    w = i * 2 + s
                    later = not isinstance(i, int) or w >= 1
                    sc, sa = ((1 - s) if half else 1), 0
                    for q in range(Q):
                        if isinstance(i, int) and w == 0:
                            pe.wait_ge(u_ready, half * NT + KQ * (q + 1))
                        if q == 3 and later:
                            transposes(job_c(half, w - 1), sc, PS_T[0], shared=True)
                        chunk(half, 1, w, s, q)
                        if q == 0 and half == 0 and later:
                            project_a(job_a(1, w - 1), w + (NT - 1), sa, 0, shared=True)
                    if later:
                        project_c(job_c(half, w - 1), sc, shared=half == 1)
                    if half == 0:
                        transposes(job_a(1, w), sa, PS_T[0], shared=True)

                if half == 0:
                    pe.wait_ge(mask_copied, NT * Q + 2)
                for s in range(2):
                    hop2(0, s)
                pairs(pe, hop2, 1)
                if half == 0:
                    project_a(job_a(1, NT - 1), 2 * NT - 1, 0, 0, shared=True)
                transposes(job_c(half, NT - 1), 1, PS_T[0], shared=True)
                project_c(job_c(half, NT - 1), 1, shared=half == 1)
                pe.wait_ge(evacuated, job_c(half, NT - 1) + 3)
                pe.wait_ge(ht_ready, job_c(half, NT - 1) + 3)
                nc.tensor.transpose(ps[0:HB * NT, PS_T[0], 0:P], s_keep[:, :, :].rearrange("p b t -> p (b t)"),
                                    ident[:, :]).then_inc(s_turned, 1)


def layer1(nc, zm, pad_dram, x1_dram, g_dram, s_dram, out):
    ctx = ExitStack()
    with ctx:
        def sb(name, shape, dt=F32):
            return ctx.enter_context(nc.sbuf_tensor(name, shape, dt))

        def sem(name):
            return ctx.enter_context(nc.semaphore(name))

        NW = 4
        PER = 3
        NB = -(-NT // PER)
        mt = mask_view(zm)
        g = sb("g", [P, 2, NT, GE])
        s_b = sb("s_b", [P, 2, N])
        wt = sb("wt", [P, NW, N])
        x1 = sb("x1", [P, 2, NT, D])
        dm = sb("dm", [P, 2, 5])
        rq = sb("rq", [P, 2, 2, NT])
        pad = sb("pad_zeros", [DMA, D])
        rden = sb("rden", [P, NT])
        ps = ctx.enter_context(nc.psum_tensor("acc", [P, NB, 512], F32))

        passed = sem("passed1")
        g_in = [sem(f"g_in{e}") for e in range(2)]
        s_in = [sem(f"s_in{e}") for e in range(2)]
        x1_in = [sem(f"x1_in{e}") for e in range(2)]
        own_max = sem("own_max")
        all_max = sem("all_max")
        guard = sem("guard")
        r_done = sem("r_done")
        factors = sem("factors")
        clipped = sem("clipped")
        t_ready = sem("t_ready")
        g_scaled = sem("g_scaled")
        w_ready = sem("w_ready")
        w_used = sem("w_used")
        bank_done = sem("bank_done")
        batch_out = sem("batch_out")
        bank_free = sem("bank_free")
        inv_done = sem("inv_done")
        stored = [sem(f"stored{e}") for e in range(2)]
        pad_ready = sem("pad_ready")

        g_v = g_dram.rearrange("h t p (b c) -> h b p t c", b=HB)
        s_v = s_dram.rearrange("h (b t) p -> h b (t p)", b=HB)
        x1_v = x1_dram.rearrange("h t p (b c) -> h b p t c", b=HB)
        out_v = out.rearrange("b (t p) f -> b p t f", p=P)

        block = ctx.enter_context(nc.Block())
        NG = NT // NW

        @block.sync
        def _(sp):
            with sp.Fori(0, 2) as half:
                with sp.Fori(0, HB // 2) as i:
                    for e in range(2):
                        b, k = half * HB + i * 2 + e, i * 2 + e
                        sp.wait_ge(bank_free, b * NB + 1)
                        sp.dma_start(g[:, e], g_v[half, k]).then_inc(g_in[e], DMA)
                        sp.dma_start(s_b[:, e, :], s_v[half, k].partition_broadcast(P)).then_inc(s_in[e], DMA)
                        sp.wait_ge(stored[e], half * (HB // 2 * DMA) + i * DMA + DMA)
                        sp.dma_start(x1[:, e], x1_v[half, k]).then_inc(x1_in[e], DMA)

        @block.gpsimd
        def _(pool):
            def reduce_max(b, e):
                wait_alone(pool, own_max, b + 1, passed)
                nc.gpsimd.partition_all_reduce(dm[:, e, 1:2], dm[:, e, 0:1], P, RMAX).then_inc(all_max, 1)

            def store(b, e):
                pool.wait_ge(bank_free, b * NB + (2 * NB + 1))
                pool.dma_start(out_v[b], x1[:, e]).then_inc(stored[e], DMA)

            nc.gpsimd.memset(pad[:, :], 0.0).then_inc(pad_ready, 1)
            pool.wait_ge(pad_ready, 1)
            for e in range(2):
                pool.dma_start(pad_dram[e], pad[:, :]).then_inc(stored[e], DMA)
            reduce_max(0, 0)
            with pool.Fori(0, B // 2 - 1) as i:
                for e in range(2):
                    reduce_max(i * 2 + (e + 1), 1 - e)
                    store(i * 2 + e, e)
            reduce_max(B - 1, 1)
            store(B - 2, 0)
            store(B - 1, 1)
            for e in range(2):
                pool.wait_ge(stored[e], B // 2 * DMA + DMA)

        @block.scalar
        def _(act):
            with act.Fori(0, B // 2) as i:
                for e in range(2):
                    b = i * 2 + e
                    act.wait_ge(guard, b * 3 + 3)
                    nc.scalar.activation(rq[:, e, 0, :], g[:, e, :, D], ACT.Exp, bias=dm[:, e, 3:4], scale=1 - SLOPE).then_inc(r_done, 1)
                    nc.scalar.activation(rq[:, e, 1, :], g[:, e, :, D], ACT.Exp, bias=dm[:, e, 4:5], scale=SLOPE).then_inc(r_done, 1)
                    act.wait_ge(r_done, b * 2 + 2)
                    nc.scalar.activation(g[:, e, :, D], g[:, e, :, D], ACT.Exp, bias=dm[:, e, 4:5],
                                         scale=SLOPE).then_inc(factors, 1)
                    act.wait_ge(clipped, b + 1)
                    nc.scalar.activation(s_b[:, e, :], s_b[:, e, :], ACT.Exp, bias=dm[:, e, 3:4],
                                         scale=SLOPE - 1).then_inc(t_ready, 1)

        @block.vector
        def _(dve):
            def own(i, e):
                dve.wait_ge(g_in[e], i * DMA + DMA)
                nc.vector.reduce_max(dm[:, e, 0:1], g[:, e, :, D], AX.X).then_inc(own_max, 1)

            def clip(i, e):
                b = i * 2 + e
                dve.wait_ge(all_max, b + 1)
                for slot, by in ((2, -1.0), (3, SLOPE - 1), (4, -SLOPE)):
                    nc.vector.tensor_scalar(dm[:, e, slot:slot + 1], dm[:, e, 1:2], by, None, ALU.mult).then_inc(guard, 1)
                dve.wait_ge(s_in[e], i * DMA + DMA)
                dve.wait_ge(guard, b * 3 + 3)
                nc.vector.tensor_scalar(s_b[:, e, :], s_b[:, e, :], dm[:, e, 2:3], None, ALU.max).then_inc(clipped, 1)

            def scale(i, e):
                dve.wait_ge(factors, i * 2 + (e + 1))
                nc.vector.tensor_tensor(g[:, e, :, 0:D], g[:, e, :, 0:D],
                                        rq[:, e, 1, :].unsqueeze(2).broadcast_to([P, NT, D]),
                                        ALU.mult).then_inc(g_scaled, 1)

            def weights(i, e, jj, slots):
                b = i * 2 + e
                dve.wait_ge(t_ready, b + 1)
                for u in slots:
                    dve.wait_ge(w_used, b * NT + jj * NW + (u + 1))
                    nc.vector.scalar_tensor_tensor(wt[:, u, :], s_b[:, e, :], rq[:, e, 0, bass.ds(jj * NW + u, 1)],
                                                   mt[:, jj * NW + u, :], ALU.max, ALU.mult).then_inc(w_ready, 1)

            def finish(i, e):
                b = i * 2 + e
                dve.wait_ge(w_used, b * NT + (NT + NW))
                for k in range(NB):
                    n = min(PER, NT - k * PER)
                    nc.vector.reciprocal(rden[:, PER * k:PER * k + n],
                                         ps[:, k, 0:n * GC].rearrange("p (n c) -> p n c", n=n)[:, :, D]).then_inc(inv_done, 1)
                dve.wait_ge(x1_in[e], i * DMA + DMA)
                dve.wait_ge(inv_done, b * NB + NB)
                for t in range(NT):
                    last = nc.vector.scalar_tensor_tensor(x1[:, e, t, :], ps[:, t // PER, GC * (t % PER):GC * (t % PER) + D],
                                                          rden[:, t:t + 1], x1[:, e, t, :], ALU.mult, ALU.add)
                    if t % PER == PER - 1 or t == NT - 1:
                        last.then_inc(bank_free, 1)

            def batch(i, e, last=False):
                nxt = (i, 1) if e == 0 else (i + 1, 0)
                weights(i, e, 0, range(NW - 1, NW))
                weights(i, e, 1, range(NW))
                if not last:
                    own(*nxt)
                weights(i, e, 2, range(NW))
                if not last:
                    clip(*nxt)
                weights(i, e, NG - 1, range(NW))
                if not last:
                    scale(*nxt)
                    weights(*nxt, 0, range(NW - 1))
                finish(i, e)

            dve.sem_inc(bank_free, NB + 1)
            own(0, 0)
            clip(0, 0)
            scale(0, 0)
            weights(0, 0, 0, range(NW - 1))
            with dve.Fori(0, B // 2 - 1) as i:
                for e in range(2):
                    batch(i, e)
            batch(B // 2 - 1, 0)
            batch(B // 2 - 1, 1, last=True)

        @block.tensor
        def _(pe):
            def group(b, e, jj, first):
                for u in range(NW):
                    pe.wait_ge(w_ready, b * NT + jj * NW + (u + 1))
                    for t in range(NT):
                        opens = first and u == 0 and t % PER == 0
                        if opens:
                            pe.wait_ge(bank_free, b * NB + (t // PER + 2))
                        col = GC * (t % PER)
                        last = nc.tensor.matmul(ps[:, t // PER, col:col + GC], wt[:, u, P * t:P * (t + 1)],
                                                g[:, e, jj * NW + u, 0:GC], start=opens, stop=True, skip_group_check=True)
                    last.then_inc(w_used, 1)

            pe.sem_inc(w_used, NW)
            with pe.Fori(0, B // 2) as i:
                for e in range(2):
                    b = i * 2 + e
                    pe.wait_ge(g_scaled, b + 1)
                    group(b, e, 0, True)
                    with pe.Fori(1, NG) as jj:
                        group(b, e, jj, False)


def build(nc, x, adj, theta, bias, gw, a_src, a_dst, out):
    pad_dram = nc.dram_tensor("pad", (2, DMA, D), F32).ap()
    z_dram = nc.dram_tensor("z_scratch", (2, 2, NT, P, W), F32).ap()
    mt_dram = nc.dram_tensor("mask_scratch", (NT, P, N), BF16).ap()
    x1_dram = nc.dram_tensor("x1_scratch", (2, NT, P, W), F32).ap()
    g_dram = nc.dram_tensor("g_scratch", (2, NT, P, HB * GE), F32).ap()
    s_dram = nc.dram_tensor("s_scratch", (2, HB * NT, P), F32).ap()
    with nc.sbuf_tensor("z_or_mask", [P, 2, NT, W], F32R) as zm:
        layer0(nc, zm, x, adj, theta, bias, gw, a_src, a_dst, z_dram, mt_dram, x1_dram, g_dram, s_dram)
        layer1(nc, zm, pad_dram, x1_dram, g_dram, s_dram, out)


INPUTS = ["x", "adj", "L0_gnn_Theta1", "L0_gnn_bias", "L1_gnn_w", "L1_gnn_a_src", "L1_gnn_a_dst"]


def kernel(**inputs):
    import numpy as np
    import concourse.bacc as bacc
    from concourse.bass_utils import run_bass_kernel_spmd

    nc = bacc.Bacc("TRN2", target_bir_lowering=False, num_devices=1)
    arrays = {f"in_{n}": np.ascontiguousarray(inputs[n]) for n in INPUTS}
    aps = [nc.dram_tensor(n, a.shape, mybir.dt.from_np(a.dtype), kind="ExternalInput").ap() for n, a in arrays.items()]
    out = nc.dram_tensor("out", (B, N, D), F32, kind="ExternalOutput").ap()
    build(nc, *aps, out)
    return run_bass_kernel_spmd(nc, [arrays], core_ids=[0]).results[0]["out"]
```

```python
import concourse.bass as bass
from concourse import mybir
from contextlib import ExitStack

F32 = mybir.dt.float32
F32R = mybir.dt.float32r
BF16 = mybir.dt.bfloat16
I32 = mybir.dt.int32
ALU = mybir.AluOpType
ACT = mybir.ActivationFunctionType
AX = mybir.AxisListType
RMAX = bass.bass_isa.ReduceOp.max

P = 128
B, N, D = 8, 2048, 128
HB = B // 2
W = HB * D
NT = N // P
Q = 4
KQ = NT // Q
EPS = 1e-5
SLOPE = 0.2
NW = 4
NG = NT // NW
PER = 3
NB = -(-NT // PER)
GC = D + 1
GE = D + 2
GB = HB - 1
SPAN = 64.0
FAR = 1e30
DMA = 16


def wait_alone(eng, sem, value, passed):
    eng.wait_ge(sem, value)
    eng.sem_inc(passed, 1)


def wait(eng, sem, value):
    if not isinstance(value, int) or value > 0:
        eng.wait_ge(sem, value)


def layers(nc, wide, x, adj, theta, bias, gw, a_src, a_dst, z_dram, mt_dram, x1_dram, g_dram, ds_dram, pad_dram, out):
    ctx = ExitStack()
    with ctx:
        def sb(name, shape, dt=F32):
            return ctx.enter_context(nc.sbuf_tensor(name, shape, dt))

        def sem(name):
            return ctx.enter_context(nc.semaphore(name))

        z = sb("z", [P, 2, NT, W], F32R)
        z_hi, z_lo = z[:, 0], z[:, 1]
        a_raw = sb("a_raw", [P, Q, KQ * P])
        a_hi = sb("a_hi", [P, Q, KQ, P], F32R)
        a_lo = sb("a_lo", [P, Q, KQ, P], F32R)
        xt = sb("xt", [P, 4, HB, D])
        h = sb("h", [P, 2, W])
        ht = sb("ht", [P, 2, W])
        zin = sb("zin", [P, 2, W])
        total = sb("total", [P, 2, W])
        z_st = sb("z_st", [P, 2, 2, W])
        g_st = sb("g_st", [P, HB, GE])
        ds_keep = sb("ds_keep", [P, 2, HB, NT])
        ds_row = sb("ds_row", [2 * HB * NT, P])
        mask = sb("mask", [P, Q, KQ * P], BF16)
        mask_t = sb("mask_t", [P, 2, KQ * P], BF16)
        ident = sb("ident", [P, P])
        ident16 = sb("ident16", [P, P], BF16)
        t_cat = sb("t_cat", [P, 3, D])
        bias_b = sb("bias_b", [P, D])
        w_ext = sb("w_ext", [P, D + 2])
        bst = sb("bst", [P, 4, HB, 6])
        mv = sb("mv", [P, 4, HB, 2])
        sd = sb("sd", [P, 4, HB])
        rstd = sb("rstd", [P, 4, HB])
        nmr = sb("nmr", [P, 4, HB])
        eps_t = sb("eps_t", [P, 1])
        eps_root = sb("eps_root", [P, 1])
        ps = ctx.enter_context(nc.psum_tensor("ps", [P, 8, 512], F32))
        acc = [ps[:, s, :] for s in range(2)]
        PS_T = (2, 0)
        PS_Z2 = (3, 1)
        PS_Z1 = (4, 6)
        PS_Z0 = (5, 7)
        PS_G = (6, 7)
        ps_m = [ps[:, 6 + e, 0:KQ * P // 2].bitcast(BF16) for e in range(2)]
        g0 = sb("g0", [P, NT, GE])
        s_b = [z_st[:, :, :, :].rearrange("p a e w -> p (a e w)"),
               a_raw[:, :, :].rearrange("p q c -> p (q c)")]
        mt = z[:, :, :, :].rearrange("p a t w -> p (a t w)").bitcast(BF16).rearrange("p (k n) -> p k n", k=NT)
        dm = sb("dm", [P, 2, 7])
        span = sb("span", [P, 2])
        rq = sb("rq", [P, 2, 2, NT])
        pad = sb("pad_zeros", [DMA, D])
        rden = sb("rden", [P, NT])
        with nc.sbuf_tensor("u", [P, 2, NT, W], F32R) as u:
            u_hi, u_lo = u[:, 0], u[:, 1]
        wt = sb("wt", [P, NW, N])
        x1_t = sb("x1_t", [P, 2, NT, D])
        g1 = sb("g1", [P, NT, GE])
        scaled = sb("scaled", [P, NT, D])
        x1 = [x1_t[:, e] for e in range(2)]
        g = [g0[:, :, :], g1[:, :, :]]

        th = z_st[:, 0].rearrange("p a w -> p (a w)")[:, 0:5 * D].rearrange("p (m d) -> p m d", m=5)
        w_t = g_st[:, 0, 0:D]
        a_cols = g_st[:, 0, D:D + 2]

        theta_in = sem("theta_in")
        w_in = sem("w_in")
        ident_ready = sem("ident_ready")
        set_up = sem("set_up")
        w_done = sem("w_done")
        passed = sem("passed")
        x_in = [sem(f"x_in{k}") for k in range(4)]
        bn_done = sem("bn_done")
        var_ready = sem("var_ready")
        sd_ready = sem("sd_ready")
        rstd_done = sem("rstd_done")
        norm_ready = sem("norm_ready")
        h_ready = sem("h_ready")
        transposed = sem("transposed")
        ht_ready = sem("ht_ready")
        projected = sem("projected")
        evacuated = sem("evacuated")
        zhi_ready = sem("zhi_ready")
        z1_staged = sem("z1_staged")
        z0_staged = sem("z0_staged")
        z_out = [[sem(f"z_out{hop}{e}") for e in range(2)] for hop in range(2)]
        ds_turned = sem("ds_turned")
        ds_staged = sem("ds_staged")
        ds_out = sem("ds_out")
        mt_first = sem("mt_first")
        mt_in = sem("mt_in")
        g_out = sem("g_out")
        a_in = [sem(f"a_in{q}") for q in range(Q)]
        hi_ready = sem("hi_ready")
        split_ready = sem("split_ready")
        chunk_used = sem("chunk_used")
        z_in = [sem(f"z_in{s}") for s in range(2)]
        summed = sem("summed")
        uhi_done = sem("uhi_done")
        u_ready = sem("u_ready")
        x1_ready = sem("x1_ready")
        x1_out = [sem(f"x1_out{s}") for s in range(2)]
        mask_ready = sem("mask_ready")
        mask_turned = sem("mask_turned")
        mask_copied = sem("mask_copied")
        mask_out = [sem(f"mask_out{e}") for e in range(2)]

        g_in = [sem(f"g_in{e}") for e in range(2)]
        s_in = [sem(f"s_in{e}") for e in range(2)]
        x1_in = [sem(f"x1_in{e}") for e in range(2)]
        own_max = sem("own_max")
        all_max = sem("all_max")
        guard = sem("guard")
        r_done = sem("r_done")
        factors = sem("factors")
        span_done = sem("span_done")
        clipped = sem("clipped")
        t_ready = sem("t_ready")
        g_scaled = sem("g_scaled")
        w_ready = sem("w_ready")
        w_used = sem("w_used")
        bank_done = sem("bank_done")
        bank_free = sem("bank_free")
        batch_out = sem("batch_out")
        part_out = sem("part_out")
        inv_done = sem("inv_done")
        stored = [sem(f"stored{e}") for e in range(2)]
        part_stored = sem("part_stored")
        pad_ready = sem("pad_ready")

        g_v = g_dram.rearrange("h t p (b c) -> h b p t c", b=HB)
        s_v = ds_dram.rearrange("h (k b t) p -> k h b (t p)", k=2, b=HB)[1]
        x1_v = x1_dram.rearrange("h t p (b c) -> h b p t c", b=HB)
        out_v = out.rearrange("b (t p) f -> b p t f", p=P)
        x_v = x.rearrange("(h b) (t p) f -> h t p b f", b=HB, p=P)
        adj_v = adj.rearrange("(k p) (w c) -> w p k c", p=P, c=P)

        def tile_no(half, hop, w):
            return (2 * half + hop) * NT + w

        def job_a(half, t):
            return t * 2 + NT if half else t

        def job_c(half, t):
            return t + 3 * NT if half else t * 2 + (NT + 1)

        def pairs(eng, body, first=0, last=NT // 2):
            with eng.Fori(first, last) as i:
                for s in range(2):
                    body(i, s)

        def quads(eng, step, between=None):
            for u in range(4):
                step(0, u)
            if between:
                between()
            with eng.Fori(1, NT // 4 - 1) as i:
                for u in range(4):
                    step(i, u)
            for u in range(4):
                step(NT // 4 - 1, u)

        def is_last(t, more):
            return isinstance(t, int) and t + more >= NT

        block = ctx.enter_context(nc.Block())

        @block.sync
        def _(sp):
            def chunks(n, w):
                for q in range(Q):
                    wait_alone(sp, split_ready, n * Q + (q + 1), passed)
                    sp.dma_start(a_raw[:, q, :].rearrange("p (k c) -> p k c", k=KQ),
                                 adj_v[w, :, KQ * q:KQ * (q + 1), :]).then_inc(a_in[q], DMA)

            def z_tile(half, hop, w, s):
                wait_alone(sp, summed, tile_no(half, hop, w) + 1, passed)
                sp.dma_start(zin[:, s, :], z_dram[half, hop, w]).then_inc(z_in[s], DMA)

            def load_gs(half, k, e):
                sp.dma_start(g[e], g_v[half, k]).then_inc(g_in[e], DMA)
                sp.dma_start(s_b[e], s_v[half, k].partition_broadcast(P)).then_inc(s_in[e], DMA)

            def load(half, k, e, seq):
                sp.wait_ge(batch_out, (half * HB + k) + 1)
                load_gs(half, k, e)
                sp.wait_ge(stored[e], seq * DMA + DMA)
                sp.dma_start(x1[e], x1_v[half, k]).then_inc(x1_in[e], DMA)

            for t in range(4):
                sp.dma_start(xt[:, t], x_v[0, t]).then_inc(x_in[t], DMA)
                if t == 0:
                    sp.dma_start(th[:, :, :], theta.rearrange("(m f) o -> f m o", f=D)).then_inc(theta_in, DMA)
                    sp.dma_start(bias_b[:, :], bias.partition_broadcast(P)).then_inc(theta_in, DMA)
            chunks(0, 0)
            sp.dma_start(w_ext[:, 0:D], gw).then_inc(w_in, DMA)
            sp.dma_start(a_cols[:, 0:1], a_dst.rearrange("(f a) -> f a", a=1)).then_inc(w_in, DMA)
            sp.dma_start(a_cols[:, 1:2], a_src.rearrange("(f a) -> f a", a=1)).then_inc(w_in, DMA)
            with sp.Fori(1, NT // 4) as i:
                for u in range(4):
                    wait_alone(sp, h_ready, i * 4 + (u - 1), passed)
                    sp.dma_start(xt[:, u], x_v[0, i * 4 + u]).then_inc(x_in[u], DMA)
            for half in range(2):
                def hop1(i, s):
                    w = i * 2 + s
                    if not is_last(w, 1):
                        chunks(tile_no(half, 0, w) + 1, w + 1)
                    else:
                        chunks(tile_no(half, 1, 0), 0)
                    z_tile(half, 0, w, s)

                def hop2(i, s):
                    w = i * 2 + s
                    if half == 0:
                        if isinstance(i, int) and i == 0:
                            sp.wait_ge(h_ready, NT + 2)
                        else:
                            wait_alone(sp, h_ready, i * 4 + (2 * s + NT - 1), passed)
                        sp.dma_start(xt[:, s], x_v[1, w]).then_inc(x_in[s], DMA)
                    if not is_last(w, 1):
                        chunks(tile_no(half, 1, w) + 1, w + 1)
                    elif half == 0:
                        chunks(tile_no(1, 0, 0), 0)
                    z_tile(half, 1, w, s)
                    if isinstance(i, int) and i == 0:
                        sp.wait_ge(h_ready, job_c(0, NT - 2 + s) + 3 if half else NT + 2)
                        wait(sp, x1_out[s], half * (NT // 2 * DMA))
                    else:
                        wait_alone(sp, h_ready, i * 2 + (3 * NT + s + 1) if half else i * 4 + (NT + 2 * s), passed)
                        wait_alone(sp, x1_out[s], i * DMA + half * (NT // 2 * DMA), passed)
                    sp.dma_start(xt[:, 2 + s], x_v[half, w]).then_inc(x_in[2 + s], DMA)
                    if half == 1:
                        if isinstance(i, int) and w == 0:
                            sp.wait_ge(chunk_used, (tile_no(1, 0, NT - 1) + 2) * Q)
                            for mask_stored in mask_out:
                                sp.wait_ge(mask_stored, NT * Q // 2 * DMA)
                        sp.dma_start(mt[:, w, :], mt_dram[w]).then_inc(mt_first if isinstance(i, int) and i == 0 else mt_in, DMA)

                for z_stored in z_out[0] + z_out[1]:
                    sp.wait_ge(z_stored, (half + 1) * (NT // 2 * DMA))
                pairs(sp, hop1, 0, NT // 2 - 1)
                if half == 1:
                    sp.wait_ge(g_out, NT * DMA)
                    sp.wait_ge(ds_out, DMA)
                    load_gs(0, 0, 0)
                for s in range(2):
                    hop1(NT // 2 - 1, s)
                for s in range(2):
                    hop2(0, s)
                pairs(sp, hop2, 1, NT // 2 - 1)
                for s in range(2):
                    hop2(NT // 2 - 1, s)

            sp.wait_ge(chunk_used, (tile_no(1, 1, NT - 1) + 2) * Q)
            for x1_stored in x1_out:
                sp.wait_ge(x1_stored, NT // 2 * DMA)
            sp.dma_start(x1[0], x1_v[0, 0]).then_inc(x1_in[0], DMA)
            for k in range(1, HB):
                load(0, k, k % 2, k // 2)
            for stored_sem, n in [(g_out, 2 * NT), (ds_out, 2)] + [(m, NT) for m in x1_out]:
                sp.wait_ge(stored_sem, n * DMA)
            with sp.Fori(0, HB // 2) as i:
                for e in range(2):
                    load(1, i * 2 + e, e, i + HB // 2)
            for k in range(0, NB, 2):
                sp.wait_ge(part_out, min(NB, k + 2))
                tiles = slice(k * PER, min(NT, (k + 2) * PER))
                sp.dma_start(out_v[B - 1][:, tiles], x1[1][:, tiles]).then_inc(part_stored, DMA)
            sp.wait_ge(part_stored, -(-NB // 2) * DMA)

        @block.gpsimd
        def _(pool):
            nc.gpsimd.memset(ident[:, :], 0.0).then_inc(ident_ready, 1)
            pool.wait_ge(ident_ready, 1)
            nc.gpsimd.affine_select(out=ident[:, :], in_=ident[:, :], compare_op=ALU.not_equal, fill=1.0,
                                    base=0, pattern=[[-1, P]], channel_multiplier=1).then_inc(ident_ready, 1)

            def reduce_max(b, e):
                wait_alone(pool, own_max, b * 2 + 2, passed)
                nc.gpsimd.partition_all_reduce(dm[:, e, 2:4], dm[:, e, 0:2], P, RMAX).then_inc(all_max, 1)

            def store(b, e):
                pool.wait_ge(batch_out, b + 3)
                pool.dma_start(out_v[b], x1[e]).then_inc(stored[e], DMA)

            def store_z(half, t, e):
                pool.wait_ge(z1_staged, t + (half * NT + 3))
                pool.dma_start(z_dram[half, 0, t], z_st[:, 0, e, :]).then_inc(z_out[0][e], DMA)
                pool.wait_ge(z0_staged, t + (half * NT + 1))
                pool.dma_start(z_dram[half, 1, t], z_st[:, 1, e, :]).then_inc(z_out[1][e], DMA)

            def store_c(half, t):
                pool.wait_ge(evacuated, job_c(half, t) + 3)
                pool.dma_start(g_dram[half, t], g_st[:, :, :].rearrange("p b c -> p (b c)")).then_inc(g_out, DMA)

            with pool.Fori(0, NT // 2) as i:
                for e in range(2):
                    store_z(0, i * 2 + e, e)
            with pool.Fori(0, NT) as w:
                for q in range(Q):
                    pool.wait_ge(mask_copied, w * Q + (q + 3))
                    pool.dma_start(mt_dram[w, :, KQ * P * q:KQ * P * (q + 1)],
                                   mask_t[:, q % 2, :]).then_inc(mask_out[q % 2], DMA)
            for half in range(2):
                def hop2(i, s):
                    w = i * 2 + s
                    if not isinstance(i, int) or w >= 2:
                        store_c(half, w - 2)
                    if half == 0 and (not isinstance(i, int) or w >= 1):
                        store_z(1, w - 1, 1 - s)
                    pool.wait_ge(x1_ready, w + (half * NT + 1))
                    pool.dma_start(x1_dram[half, w], xt[:, 2 + s].rearrange("p b f -> p (b f)")).then_inc(x1_out[s], DMA)

                if half == 1:
                    reduce_max(0, 0)
                for s in range(2):
                    hop2(0, s)
                pairs(pool, hop2, 1)
                store_c(half, NT - 2)
                if half == 0:
                    store_z(1, NT - 1, 1)
                store_c(half, NT - 1)
                pool.wait_ge(ds_staged, half + 1)
                pool.dma_start(ds_dram[half], ds_row[:, :]).then_inc(ds_out, DMA)
            nc.gpsimd.memset(pad[:, :], 0.0).then_inc(pad_ready, 1)
            pool.wait_ge(pad_ready, 1)
            for e in range(2):
                pool.dma_start(pad_dram[e], pad[:, :]).then_inc(stored[e], DMA)
            with pool.Fori(0, B // 2 - 1) as i:
                for e in range(2):
                    reduce_max(i * 2 + (e + 1), 1 - e)
                    store(i * 2 + e, e)
            reduce_max(B - 1, 1)
            store(B - 2, 0)
            for e in range(2):
                pool.wait_ge(stored[e], (B // 2 - e) * DMA + DMA)

        @block.scalar
        def _(act):
            def high(n, q):
                act.wait_ge(a_in[q], n * DMA + DMA)
                act.wait_ge(chunk_used, n * Q + (q + 1))
                nc.scalar.activation(a_hi[:, q].rearrange("p k c -> p (k c)"), a_raw[:, q, :],
                                     ACT.Copy).then_inc(hi_ready, 1)

            def turned(w, q):
                act.wait_ge(mask_turned, w * Q + (q + 1 + Q))
                wait(act, mask_out[q % 2], w * (Q // 2 * DMA) + q // 2 * DMA)
                nc.scalar.activation(mask_t[:, q % 2, :], ps_m[q % 2], ACT.Copy).then_inc(mask_copied, 1)

            def deviation(v, s):
                act.wait_ge(var_ready, v + 1)
                nc.scalar.activation(sd[:, s, :], mv[:, s, :, 1], ACT.Sqrt, bias=eps_t[:, :]).then_inc(sd_ready, 1)

            def normalise(v, s, slot, st=None):
                st = s if st is None else st
                act.wait_ge(norm_ready, v + 1)
                act.wait_ge(transposed, v + 1)
                for b in range(HB):
                    done = nc.scalar.activation(h[:, s, D * b:D * (b + 1)], xt[:, slot, b, :], ACT.Relu,
                                                bias=nmr[:, st, b:b + 1], scale=rstd[:, st, b:b + 1])
                done.then_inc(h_ready, 1)

            def copy_ht(v, s, bank):
                act.wait_ge(transposed, v + 3)
                act.wait_ge(projected, v + 1)
                nc.scalar.activation(ht[:, s, :], ps[:, bank, :], ACT.Copy).then_inc(ht_ready, 1)

            def high_z(v, t, k):
                act.wait_ge(projected, v + 3)
                nc.scalar.activation(z_hi[:, t], ps[:, PS_Z2[k], :], ACT.Copy).then_inc(zhi_ready, 1)

            def stage_z1(k, e, stored):
                wait(act, z_out[0][e], stored * DMA)
                nc.scalar.activation(z_st[:, 0, e, :], ps[:, PS_Z1[k], :], ACT.Copy).then_inc(z1_staged, 1)

            def factor(i, e):
                b = i * 2 + e
                act.wait_ge(guard, b * 3 + 3)
                nc.scalar.activation(rq[:, e, 0, :], g[e][:, :, D], ACT.Exp, bias=dm[:, e, 5:6], scale=1 - SLOPE).then_inc(r_done, 1)
                nc.scalar.activation(rq[:, e, 1, :], g[e][:, :, D], ACT.Exp, bias=dm[:, e, 6:7], scale=SLOPE).then_inc(r_done, 1)
                act.wait_ge(r_done, b * 2 + 2)
                nc.scalar.activation(g[e][:, :, D], g[e][:, :, D], ACT.Exp, bias=dm[:, e, 6:7],
                                     scale=SLOPE).then_inc(factors, 1)
                act.wait_ge(clipped, b + 1)
                nc.scalar.activation(s_b[e], s_b[e], ACT.Exp, bias=dm[:, e, 5:6],
                                     scale=SLOPE - 1).then_inc(t_ready, 1)

            for ring in (h_ready, ht_ready, z1_staged, mask_copied):
                act.sem_inc(ring, 2)
            act.sem_inc(bank_free, NB + 1)
            act.wait_ge(set_up, 1)
            nc.scalar.activation(eps_root[:, :], eps_t[:, :], ACT.Sqrt)

            deviation(0, 0)
            normalise(0, 0, 0)
            deviation(1, 1)
            normalise(1, 1, 1)
            deviation(2, 2)
            copy_ht(0, 0, PS_T[0])

            def step(i, u):
                t = i * 4 + u
                if not isinstance(t, int) or t >= 1:
                    high_z(t - 1, t - 1, (u + 1) % 2)
                if not is_last(t, 2):
                    normalise(t + 2, u % 2, (u + 2) % 4, (u + 2) % 4)
                if not is_last(t, 1):
                    copy_ht(t + 1, (u + 1) % 2, PS_T[(u + 1) % 2])
                if not is_last(t, 3):
                    deviation(t + 3, (u + 3) % 4)
                if not isinstance(t, int) or t >= 1:
                    stage_z1((u + 1) % 2, (u + 1) % 2, i * 2 + (u - 1) // 2)

            quads(act, step, lambda: [high(0, q) for q in range(Q)])
            high_z(NT - 1, NT - 1, 1)
            stage_z1(1, 1, NT // 2 - 1)

            for half in range(2):
                def hop1(w):
                    for q in range(Q):
                        high(tile_no(half, 0, w) + 1, q)
                        if half == 0:
                            turned(w, q)

                hop1(0)
                with act.Fori(1, NT) as w:
                    hop1(w)

                if half == 1:
                    factor(0, 0)

                def hop2(i, s):
                    w = i * 2 + s
                    later = not isinstance(i, int) or w >= 1
                    last = half == 1 and is_last(w, 1)
                    sc, sa = ((1 - s) % 2 if half else 1), 0
                    if not last:
                        high(tile_no(half, 1, w) + 1, 0)
                    if later:
                        deviation(job_c(half, w - 1), sc)
                        normalise(job_c(half, w - 1), sc, 2 + (1 - s))
                    if not last:
                        high(tile_no(half, 1, w) + 1, 1)
                    if half == 0:
                        if later:
                            high_z(job_a(1, w - 1), w - 1, 0)
                            stage_z1(0, 1 - s, i + (NT // 2 + s - 1))
                        deviation(job_a(1, w), sa)
                        normalise(job_a(1, w), sa, s)
                    if not last:
                        high(tile_no(half, 1, w) + 1, 2)
                    if later:
                        copy_ht(job_c(half, w - 1), sc, PS_T[0])
                    if not last:
                        high(tile_no(half, 1, w) + 1, 3)
                    if half == 0:
                        copy_ht(job_a(1, w), sa, PS_T[0])

                for s in range(2):
                    hop2(0, s)
                pairs(act, hop2, 1, NT // 2 - 1)
                for s in range(2):
                    hop2(NT // 2 - 1, s)
                v = job_c(half, NT - 1)
                deviation(v, v % 2)
                normalise(v, v % 2, 3)
                if half == 0:
                    high_z(job_a(1, NT - 1), NT - 1, 0)
                    stage_z1(0, 1, NT - 1)
                copy_ht(v, v % 2, PS_G[0] if half else PS_T[0])

            def divide(i, e):
                b = i * 2 + e
                act.wait_ge(batch_out, b + 2)
                for k in range(NB):
                    act.wait_ge(inv_done, b * NB + (k + 1))
                    for t in range(k * PER, min(NT, (k + 1) * PER)):
                        col = GC * (t - k * PER)
                        last = nc.scalar.activation(scaled[:, t, :], ps[:, k, col:col + D], ACT.Copy, scale=rden[:, t:t + 1])
                    last.then_inc(bank_free, 1)

            with act.Fori(0, B // 2 - 1) as i:
                for e in range(2):
                    factor(i + e, 1 - e)
                    divide(i, e)
            factor(B // 2 - 1, 1)
            divide(B // 2 - 1, 0)
            divide(B // 2 - 1, 1)

        @block.vector
        def _(dve):
            def low(n, q, w=None):
                dve.wait_ge(hi_ready, n * Q + (q + 1))
                if w is not None:
                    dve.wait_ge(mask_turned, w * Q + (q + 1))
                    nc.vector.tensor_scalar(mask[:, q, :], a_raw[:, q, :], 0.0, None, ALU.is_gt).then_inc(mask_ready, 1)
                nc.vector.tensor_tensor(a_lo[:, q].rearrange("p k c -> p (k c)"), a_raw[:, q, :],
                                        a_hi[:, q].rearrange("p k c -> p (k c)").bitcast(F32),
                                        ALU.subtract).then_inc(split_ready, 1)

            def add_z(half, hop, i, s):
                n = tile_no(half, hop, i * 2 + s)
                dve.wait_ge(z_in[s], i * DMA + ((2 * half + hop) * (NT // 2) + 1) * DMA)
                dve.wait_ge(chunk_used, n * Q + 2 * Q)
                nc.vector.tensor_tensor(total[:, s, :], acc[s], zin[:, s, :], ALU.add).then_inc(summed, 1)
                wait_alone(dve, summed, n + 3, passed)

            def end_hop1(half, i, s):
                add_z(half, 0, i, s)
                w = i * 2 + s
                nc.vector.tensor_copy(u_hi[:, w], total[:, s, :]).then_inc(uhi_done, 1)
                dve.wait_ge(uhi_done, w + (half * NT + 1))
                nc.vector.tensor_tensor(u_lo[:, w], total[:, s, :], u_hi[:, w].bitcast(F32),
                                        ALU.subtract).then_inc(u_ready, 1)

            def stats(v, s, slot, ring=2):
                wait(dve, h_ready, v + 3 - ring if isinstance(v, int) else v + (3 - ring))
                for b in range(HB):
                    last = nc.vector.bn_stats(bst[:, s, b, :], xt[:, slot, b, :])
                last.then_inc(bn_done, 1)
                wait_alone(dve, bn_done, v + 1, passed)
                for b in range(HB):
                    last = nc.vector.bn_aggr(mv[:, s, b, :], bst[:, s, b, :])
                last.then_inc(var_ready, 1)

            def norms(v, s):
                dve.wait_ge(sd_ready, v + 1)
                nc.vector.reciprocal(rstd[:, s, :], sd[:, s, :]).then_inc(rstd_done, 1)
                dve.wait_ge(rstd_done, v + 1)
                nc.vector.scalar_tensor_tensor(nmr[:, s, :], mv[:, s, :, 0], -1.0, rstd[:, s, :],
                                               ALU.mult, ALU.mult).then_inc(norm_ready, 1)

            def stage_z0(v, k, e, stored):
                dve.wait_ge(projected, v + 3)
                wait(dve, z_out[1][e], stored * DMA)
                z0 = ps[:, PS_Z0[k], :].rearrange("p (b f) -> p b f", b=HB)
                nc.vector.tensor_tensor(z_st[:, 1, e, :].rearrange("p (b f) -> p b f", b=HB), z0,
                                        bias_b[:, :].unsqueeze(1).broadcast_to([P, HB, D]), ALU.add).then_inc(z0_staged, 1)

            def low_z(a, t, k):
                dve.wait_ge(zhi_ready, a + 1)
                nc.vector.tensor_tensor(z_lo[:, t], ps[:, PS_Z2[k], :], z_hi[:, t].bitcast(F32),
                                        ALU.subtract).then_inc(evacuated, 1)

            def evacuate_c(half, t):
                dve.wait_ge(projected, job_c(half, t) + 3)
                wait(dve, g_out, t * DMA + half * (NT * DMA))
                nc.vector.tensor_copy(g_st[:, 0:GB, :].rearrange("p b c -> p (b c)"), ps[:, PS_G[0], 0:GB * GE])
                nc.vector.tensor_copy(g_st[:, GB, :], ps[:, PS_G[1], 0:GE])
                wait(dve, ds_turned, half)
                nc.vector.tensor_copy(ds_keep[:, :, 0:GB, t].rearrange("p k b -> p b k"),
                                      ps[:, PS_G[0], 0:GB * GE].rearrange("p (b c) -> p b c", c=GE)[:, :, D:GE])
                nc.vector.tensor_copy(ds_keep[:, :, GB, t], ps[:, PS_G[1], D:GE]).then_inc(evacuated, 1)

            def own(i, e):
                dve.wait_ge(g_in[e], i * DMA + DMA)
                nc.vector.reduce_max(dm[:, e, 0:1], g[e][:, :, D], AX.X).then_inc(own_max, 1)
                nc.vector.tensor_reduce(dm[:, e, 1:2], g[e][:, :, D], AX.X, ALU.min, negate=True).then_inc(own_max, 1)

            def clip(i, e):
                b = i * 2 + e
                dve.wait_ge(all_max, b + 1)
                for slot, by in ((4, -1.0), (5, SLOPE - 1), (6, -SLOPE)):
                    nc.vector.tensor_scalar(dm[:, e, slot:slot + 1], dm[:, e, 2:3], by, None, ALU.mult).then_inc(guard, 1)
                nc.vector.tensor_tensor(span[:, 0:1], dm[:, e, 2:3], dm[:, e, 3:4], ALU.add).then_inc(span_done, 1)
                dve.wait_ge(span_done, b * 2 + 2)
                nc.vector.tensor_tensor(span[:, 1:2], span[:, 1:2], span[:, 0:1], ALU.max).then_inc(span_done, 1)
                dve.wait_ge(s_in[e], i * DMA + DMA)
                dve.wait_ge(guard, b * 3 + 3)
                nc.vector.tensor_scalar(s_b[e], s_b[e], dm[:, e, 4:5], None, ALU.max).then_inc(clipped, 1)

            def scale(i, e):
                dve.wait_ge(factors, i * 2 + (e + 1))
                nc.vector.tensor_tensor(g[e][:, :, 0:D], g[e][:, :, 0:D],
                                        rq[:, e, 1, :].unsqueeze(2).broadcast_to([P, NT, D]),
                                        ALU.mult).then_inc(g_scaled, 1)

            def weights(i, e, jj, slots):
                b = i * 2 + e
                dve.wait_ge(t_ready, b + 1)
                for u in slots:
                    dve.wait_ge(w_used, b * NT + jj * NW + (u + 1))
                    nc.vector.scalar_tensor_tensor(wt[:, u, :], s_b[e], rq[:, e, 0, bass.ds(jj * NW + u, 1)],
                                                   mt[:, jj * NW + u, :], ALU.max, ALU.mult).then_inc(w_ready, 1)

            def finish(i, e, last):
                b = i * 2 + e
                dve.wait_ge(x1_in[e], i * DMA + DMA)

                def add(k):
                    dve.wait_ge(bank_free, b * NB + (NB + k + 2))
                    tiles = slice(k * PER, min(NT, (k + 1) * PER))
                    nc.vector.tensor_tensor(x1[e][:, tiles], scaled[:, tiles, :], x1[e][:, tiles], ALU.add).then_inc(part_out, 1)

                for k in range(NB):
                    first, n = k * PER, min(PER, NT - k * PER)
                    if k < NB - 1:
                        dve.wait_ge(bank_done, b * (NB - 1) + (k + 1))
                    else:
                        dve.wait_ge(w_used, b * NT + (NT + NW))
                    nc.vector.reciprocal(rden[:, first:first + n],
                                         ps[:, k, 0:n * GC].rearrange("p (n c) -> p n c", n=n)[:, :, D]).then_inc(inv_done, 1)
                    if last and k >= 2:
                        add(k - 2)
                if last:
                    add(NB - 2)
                    add(NB - 1)
                else:
                    dve.wait_ge(bank_free, b * NB + (2 * NB + 1))
                    nc.vector.tensor_tensor(x1[e], scaled[:, :, :], x1[e], ALU.add).then_inc(batch_out, 1)

            def batch(i, e, last=False):
                nxt = (i, 1) if e == 0 else (i + 1, 0)
                weights(i, e, 1, range(NW))
                if not last:
                    own(*nxt)
                weights(i, e, 2, range(NW))
                if not last:
                    clip(*nxt)
                weights(i, e, NG - 1, range(NW))
                if not last:
                    scale(*nxt)
                    weights(*nxt, 0, range(NW - 1))
                finish(i, e, last)
                if not last:
                    weights(*nxt, 0, range(NW - 1, NW))

            dve.sem_inc(batch_out, 2)
            nc.vector.memset(span[:, 1:2], 0.0).then_inc(span_done, 1)
            dve.sem_inc(evacuated, 2)
            dve.sem_inc(summed, 2)
            dve.sem_inc(split_ready, Q)
            nc.vector.memset(eps_t[:, :], EPS).then_inc(set_up, 1)
            dve.wait_ge(ident_ready, 2)
            nc.vector.tensor_copy(ident16[:, :], ident[:, :]).then_inc(set_up, 1)
            def ahead(i, u):
                dve.wait_ge(x_in[u % 4], i * DMA + (u // 4 + 1) * DMA)
                stats(i * 4 + u, u % 4, u % 4, ring=4)

            def step(i, u):
                t = i * 4 + u
                if not is_last(t, 2):
                    norms(t + 2, (u + 2) % 4)
                if not is_last(t, 3):
                    ahead(i, u + 3)
                if not isinstance(t, int) or t >= 1:
                    stage_z0(t - 1, (u + 1) % 2, (u + 1) % 2, i * 2 + (u - 1) // 2)
                    low_z(t - 1, t - 1, (u + 1) % 2)

            ahead(0, 0)
            ahead(0, 1)
            norms(0, 0)
            norms(1, 1)
            dve.wait_ge(theta_in, 2 * DMA)
            nc.vector.tensor_tensor(t_cat[:, 0, :], th[:, 2, :], th[:, 4, :], ALU.add).then_inc(set_up, 1)
            nc.vector.tensor_tensor(t_cat[:, 1, :], th[:, 1, :], th[:, 3, :], ALU.add).then_inc(set_up, 1)
            dve.wait_ge(set_up, 3)
            nc.vector.tensor_tensor(t_cat[:, 2, :], th[:, 0, :], t_cat[:, 0, :], ALU.subtract).then_inc(set_up, 1)
            dve.wait_ge(set_up, 5)
            nc.vector.tensor_scalar(t_cat[:, 0, :], t_cat[:, 0, :], 2.0, None, ALU.mult).then_inc(set_up, 1)
            ahead(0, 2)
            quads(dve, step, lambda: [low(0, q, 0) for q in range(Q)])
            stage_z0(NT - 1, 1, 1, NT // 2 - 1)
            low_z(NT - 1, NT - 1, 1)
            dve.wait_ge(w_done, 1)
            nc.vector.tensor_copy(w_t, ps[:, PS_T[0], 0:D]).then_inc(set_up, 1)

            for half in range(2):
                def hop1(i, s):
                    w = i * 2 + s
                    for q in range(Q):
                        low(tile_no(half, 0, w) + 1, q, w + 1 if half == 0 and not is_last(w, 1) else None)
                    end_hop1(half, i, s)

                pairs(dve, hop1, 0, NT // 2 - 1)
                for s in range(2):
                    hop1(NT // 2 - 1, s)

                def hop2(i, s):
                    w = i * 2 + s
                    later, second = (not isinstance(i, int) or w >= k for k in (1, 2))
                    last = half == 1 and is_last(w, 1)
                    sc, sa = ((1 - s) if half else 1), 0
                    if not last:
                        low(tile_no(half, 1, w) + 1, 0)
                    if later:
                        norms(job_c(half, w - 1), sc)
                    if half == 0:
                        dve.wait_ge(x_in[s], i * DMA + (NT // 4 + 1) * DMA)
                        stats(job_a(1, w), sa, s)
                    if second:
                        evacuate_c(half, w - 2)
                    if not last:
                        low(tile_no(half, 1, w) + 1, 1)
                    if half == 0:
                        if later:
                            stage_z0(job_a(1, w - 1), 0, 1 - s, i + (NT // 2 + s - 1))
                            low_z(w + (NT - 1), w - 1, 0)
                        norms(job_a(1, w), sa)
                    if not last:
                        low(tile_no(half, 1, w) + 1, 2)
                        low(tile_no(half, 1, w) + 1, 3)
                    else:
                        dve.wait_ge(mt_first, 2 * DMA)
                        dve.wait_ge(chunk_used, tile_no(1, 1, w) * Q + Q + 2)
                        weights(0, 0, 0, range(2))
                    add_z(half, 1, i, s)
                    dve.wait_ge(x_in[2 + s], i * DMA + (NT // 4 + half * (NT // 2) + 1) * DMA)
                    xs = xt[:, 2 + s].rearrange("p b f -> p (b f)")
                    nc.vector.scalar_tensor_tensor(xs, total[:, s, :], 0.0, xs, ALU.max, ALU.add).then_inc(x1_ready, 1)
                    dve.wait_ge(x1_ready, w + (half * NT + 1))
                    stats(job_c(half, w), s if half else 1, 2 + s)

                if half == 1:
                    own(0, 0)
                    clip(0, 0)
                    scale(0, 0)
                if half == 0:
                    dve.wait_ge(w_done, 2)
                    nc.vector.tensor_copy(w_ext[:, D:D + 2], ps[:, PS_Z2[0], 0:2]).then_inc(set_up, 1)
                for i in range(2):
                    for s in range(2):
                        hop2(i, s)
                pairs(dve, hop2, 2, NT // 2 - 1)
                for s in range(2):
                    hop2(NT // 2 - 1, s)
                norms(job_c(half, NT - 1), 1)
                evacuate_c(half, NT - 2)
                if half == 0:
                    stage_z0(job_a(1, NT - 1), 0, 1, NT - 1)
                    low_z(2 * NT - 1, NT - 1, 0)
                else:
                    dve.wait_ge(mt_in, (NT - 2) * DMA)
                    weights(0, 0, 0, range(2, NW - 1))
                evacuate_c(half, NT - 1)
                if half == 1:
                    weights(0, 0, 0, range(NW - 1, NW))
                dve.wait_ge(ds_turned, half + 1)
                wait(dve, ds_out, half * DMA)
                nc.vector.tensor_copy(ds_row[:, :], ps[:, PS_G[1], 0:P]).then_inc(ds_staged, 1)

            with dve.Fori(0, B // 2 - 1) as i:
                for e in range(2):
                    batch(i, e)
            batch(B // 2 - 1, 0)
            batch(B // 2 - 1, 1, last=True)
            dve.wait_ge(span_done, 2 * B + 1)
            nc.vector.tensor_scalar(wide[:, :], span[:, 1:2], SPAN, None, ALU.is_gt)

        @block.tensor
        def _(pe):
            def transposes(v, s, bank, shared=False):
                pe.wait_ge(h_ready, v + 3)
                pe.wait_ge(ht_ready, v + 1 + shared)
                for b in range(HB):
                    last = nc.tensor.transpose(ps[:, bank, D * b:D * (b + 1)], h[:, s, D * b:D * (b + 1)], ident[:, :])
                last.then_inc(transposed, 1)

            def project_a(v, a, s, k, shared=False):
                pe.wait_ge(ht_ready, v + 3)
                pe.wait_ge(evacuated, v + 1)
                pe.wait_ge(z1_staged, a + 1 + shared)
                for b in range(HB):
                    h_t = ht[:, s, D * b:D * (b + 1)]
                    for m, bank in enumerate((PS_Z2[k], PS_Z1[k], PS_Z0[k])):
                        last = nc.tensor.matmul(ps[:, bank, D * b:D * (b + 1)], h_t, t_cat[:, m, :], start=True, stop=True)
                last.then_inc(projected, 1)

            def project_c(v, s, shared):
                pe.wait_ge(ht_ready, v + 3)
                pe.wait_ge(evacuated, v + 1 + shared)
                for b in range(HB):
                    col = GE * (b % GB)
                    last = nc.tensor.matmul(ps[:, PS_G[b // GB], col:col + GE], ht[:, s, D * b:D * (b + 1)], w_ext[:, :],
                                            start=True, stop=True)
                last.then_inc(projected, 1)

            def turn_ds(half):
                pe.wait_ge(evacuated, job_c(half, NT - 1) + 3)
                nc.tensor.transpose(ps[:, PS_G[1], 0:P], ds_keep[:, :, :, :].rearrange("p k b t -> p (k b t)"),
                                    ident[:, :]).then_inc(ds_turned, 1)

            def chunk(half, hop, w, s, q):
                n = tile_no(half, hop, w)
                hi, lo = (u_hi, u_lo) if hop else (z_hi, z_lo)
                if q == 0:
                    pe.wait_ge(summed, n + 1)
                pe.wait_ge(split_ready, n * Q + (q + 1 + Q))
                for kk in range(KQ):
                    k = q * KQ + kk
                    nc.tensor.matmul(acc[s], a_hi[:, q, kk, :], hi[:, k, :], start=k == 0, stop=False)
                    nc.tensor.matmul(acc[s], a_hi[:, q, kk, :], lo[:, k, :], start=False, stop=False)
                    last = nc.tensor.matmul(acc[s], a_lo[:, q, kk, :], hi[:, k, :], start=False, stop=k == NT - 1)
                last.then_inc(chunk_used, 1)

            def group(b, e, jj, first=False, final=False, slots=range(NW)):
                for u in slots:
                    pe.wait_ge(w_ready, b * NT + jj * NW + (u + 1))
                    for t in range(NT):
                        opens = first and u == 0 and t % PER == 0
                        if opens:
                            pe.wait_ge(bank_free, b * NB + (t // PER + 2))
                        col = GC * (t % PER)
                        last = nc.tensor.matmul(ps[:, t // PER, col:col + GC], wt[:, u, P * t:P * (t + 1)],
                                                g[e][:, jj * NW + u, 0:GC], start=opens, stop=True, skip_group_check=True)
                        if final and u == NW - 1 and t % PER == PER - 1:
                            last.then_inc(bank_done, 1)
                    last.then_inc(w_used, 1)

            pe.sem_inc(w_used, NW)
            pe.sem_inc(transposed, 2)
            pe.sem_inc(projected, 2)
            pe.sem_inc(chunk_used, Q)
            pe.sem_inc(mask_turned, Q)
            pe.wait_ge(ident_ready, 2)

            def step(i, u):
                t = i * 4 + u
                if not is_last(t, 1):
                    transposes(t + 1, (u + 1) % 2, PS_T[(u + 1) % 2])
                project_a(t, t, u % 2, u % 2)

            transposes(0, 0, PS_T[0])
            pe.wait_ge(set_up, 6)
            quads(pe, step)
            pe.wait_ge(w_in, 3 * DMA)
            nc.tensor.transpose(ps[:, PS_T[0], 0:D], w_ext[:, 0:D], ident[:, :]).then_inc(w_done, 1)
            for half in range(2):
                def hop1(i, s):
                    w = i * 2 + s
                    first = isinstance(i, int) and w == 0
                    between = half == 1 and first
                    for q in range(Q):
                        if first:
                            pe.wait_ge(evacuated, job_a(half, KQ * (q + 1) - 1) + 3)
                        chunk(half, 0, w, s, q)
                        if between and q == 1:
                            transposes(job_c(0, NT - 1), 1, PS_T[0], shared=True)
                            project_c(job_c(0, NT - 1), 1, shared=False)
                        if between and q == 2:
                            turn_ds(0)
                        if half == 0:
                            if first and q == 0:
                                pe.wait_ge(evacuated, job_a(0, NT - 1) + 3)
                                pe.wait_ge(z1_staged, NT + 2)
                            pe.wait_ge(mask_ready, w * Q + (q + 1))
                            pe.wait_ge(mask_copied, w * Q + (q + 1))
                            for kk in range(KQ):
                                last = nc.tensor.transpose(ps_m[q % 2][:, P * kk:P * (kk + 1)],
                                                           mask[:, q, P * kk:P * (kk + 1)], ident16[:, :])
                            last.then_inc(mask_turned, 1)

                for s in range(2):
                    hop1(0, s)
                pairs(pe, hop1, 1)

                def hop2(i, s):
                    w = i * 2 + s
                    later = not isinstance(i, int) or w >= 1
                    sc, sa = ((1 - s) if half else 1), 0
                    for q in range(Q):
                        if isinstance(i, int) and w == 0:
                            pe.wait_ge(u_ready, half * NT + KQ * (q + 1))
                        if q == 3 and later:
                            transposes(job_c(half, w - 1), sc, PS_T[0], shared=True)
                        chunk(half, 1, w, s, q)
                        if q == 0 and half == 0 and later:
                            project_a(job_a(1, w - 1), w + (NT - 1), sa, 0, shared=True)
                    if later:
                        project_c(job_c(half, w - 1), sc, shared=half == 1)
                    if half == 0:
                        transposes(job_a(1, w), sa, PS_T[0], shared=True)

                if half == 0:
                    pe.wait_ge(set_up, 7)
                    nc.tensor.matmul(ps[:, PS_Z2[0], 0:2], w_t, a_cols, start=True, stop=True).then_inc(w_done, 1)
                    pe.wait_ge(mask_copied, NT * Q + 2)
                for s in range(2):
                    hop2(0, s)
                    if half == 0 and s == 0:
                        pe.wait_ge(set_up, 8)
                pairs(pe, hop2, 1)
                if half == 0:
                    project_a(job_a(1, NT - 1), 2 * NT - 1, 0, 0, shared=True)
                if half == 1:
                    pe.wait_ge(summed, tile_no(1, 1, NT - 1) + 3)
                    pe.wait_ge(g_scaled, 1)
                    group(0, 0, 0, first=True, slots=range(2))
                    pe.wait_ge(evacuated, job_c(half, NT - 2) + 3)
                    transposes(job_c(1, NT - 1), 1, PS_G[0], shared=True)
                    project_c(job_c(1, NT - 1), 1, shared=True)
                    group(0, 0, 0, first=True, slots=range(2, 3))
                    turn_ds(1)
            group(0, 0, 0, first=True, slots=range(3, NW))

            def rest(b, e):
                with pe.Fori(1, NG - 1) as jj:
                    group(b, e, jj)
                group(b, e, NG - 1, final=True)

            def batch(b, e):
                pe.wait_ge(g_scaled, b + 1)
                group(b, e, 0, first=True)
                rest(b, e)

            rest(0, 0)
            with pe.Fori(0, B // 2 - 1) as i:
                for e in range(2):
                    batch(i * 2 + (e + 1), 1 - e)
            batch(B - 1, 1)


def layer1_wide(nc, wide, adj, x1_dram, g_dram, ds_dram, out):
    ctx = ExitStack()
    with ctx:
        def sb(name, shape, dt=F32):
            return ctx.enter_context(nc.sbuf_tensor(name, shape, dt))

        def sem(name):
            return ctx.enter_context(nc.semaphore(name))

        CH = 512 // P
        g_all = sb("g_wide", [P, NT, GE])
        d_b = sb("d_rows", [P, N])
        am = sb("adj_rows", [P, N])
        far = sb("far", [P, N])
        e = sb("scores", [P, N])
        et = sb("weights_t", [P, NT, P])
        x1 = sb("x1_rows", [P, D])
        ident = sb("ident_wide", [P, P])
        neg = sb("neg_max", [P, 1])
        den = sb("den", [P, 2])
        ps = ctx.enter_context(nc.psum_tensor("wide_ps", [P, 8, 512], F32))
        ident_made = sem("ident_made")
        batch_in = sem("batch_in")
        rows_in = sem("rows_in")
        score_step = sem("score_step")
        weights_made = sem("weights_made")
        masked = sem("masked")
        turned = sem("turned")
        copied = sem("copied")
        products = sem("products")
        result = sem("result")
        result_out = sem("result_out")
        result_seen = sem("result_seen")
        STEPS = 7

        x1_v = x1_dram.rearrange("h t p (b c) -> h b t p c", b=HB)
        g_v = g_dram.rearrange("h t p (b c) -> h b p t c", b=HB)
        d_v = ds_dram.rearrange("h (k b t) p -> k h b (t p)", k=2, b=HB)[0]
        adj_v = adj.rearrange("(t p) n -> t p n", p=P)
        out_v = out.rearrange("(h b) (t p) f -> h b t p f", b=HB, p=P)

        block = ctx.enter_context(nc.Block())

        def where_wide(eng, body):
            flag = eng.value_load(wide[0:1, 0:1], min_val=0, max_val=1)
            with eng.If(flag > 0):
                with eng.Fori(0, 2) as half:
                    with eng.Fori(0, HB) as k:
                        body(half, k)

        @block.sync
        def _(sp):
            def batch(half, k):
                sp.dma_start(g_all[:, :, :], g_v[half, k]).then_inc(batch_in, DMA)
                sp.dma_start(d_b[:, :], d_v[half, k].partition_broadcast(P)).then_inc(batch_in, DMA)
                with sp.Fori(0, NT) as t:
                    n = (half * HB + k) * NT + t
                    sp.dma_start(am[:, :], adj_v[t]).then_inc(rows_in, DMA)
                    sp.dma_start(x1[:, :], x1_v[half, k, t]).then_inc(rows_in, DMA)
                    sp.wait_ge(result, n + 1)
                    sp.dma_start(out_v[half, k, t], x1[:, :]).then_inc(result_out, DMA)
                    wait_alone(sp, result_out, n * DMA + DMA, result_seen)

            where_wide(sp, batch)

        @block.gpsimd
        def _(pool):
            nc.gpsimd.memset(ident[:, :], 0.0).then_inc(ident_made, 1)
            pool.wait_ge(ident_made, 1)
            nc.gpsimd.affine_select(out=ident[:, :], in_=ident[:, :], compare_op=ALU.not_equal, fill=1.0,
                                    base=0, pattern=[[-1, P]], channel_multiplier=1).then_inc(ident_made, 1)

        @block.scalar
        def _(act):
            def batch(half, k):
                with act.Fori(0, NT) as t:
                    n = (half * HB + k) * NT + t
                    act.wait_ge(score_step, n * STEPS + STEPS)
                    nc.scalar.activation(e[:, :], e[:, :], ACT.Exp, bias=neg[:, :]).then_inc(weights_made, 1)

            where_wide(act, batch)

        @block.vector
        def _(dve):
            def batch(half, k):
                with dve.Fori(0, NT) as t:
                    n = (half * HB + k) * NT + t

                    def step(number, instruction):
                        instruction.then_inc(score_step, 1)
                        dve.wait_ge(score_step, n * STEPS + number)

                    dve.wait_ge(batch_in, half * (2 * HB * DMA) + k * (2 * DMA) + 2 * DMA)
                    dve.wait_ge(rows_in, n * (2 * DMA) + 2 * DMA)
                    step(1, nc.vector.tensor_scalar(e[:, :], d_b[:, :], g_all[:, bass.ds(t, 1), D + 1], None, ALU.add))
                    step(2, nc.vector.scalar_tensor_tensor(e[:, :], e[:, :], SLOPE, e[:, :], ALU.mult, ALU.max))
                    step(3, nc.vector.tensor_scalar(am[:, :], am[:, :], 0.0, None, ALU.is_gt))
                    step(4, nc.vector.tensor_scalar(far[:, :], am[:, :], 1.0, FAR, ALU.subtract, ALU.mult))
                    step(5, nc.vector.tensor_tensor(e[:, :], e[:, :], am[:, :], ALU.mult))
                    step(6, nc.vector.tensor_tensor(e[:, :], e[:, :], far[:, :], ALU.add))
                    nc.vector.tensor_reduce(neg[:, :], e[:, :], AX.X, ALU.max, negate=True).then_inc(score_step, 1)
                    dve.wait_ge(weights_made, n + 1)
                    nc.vector.tensor_tensor(e[:, :], e[:, :], am[:, :], ALU.mult).then_inc(masked, 1)
                    dve.wait_ge(masked, n * 3 + 1)
                    nc.vector.reduce_sum(den[:, 0:1], e[:, :], AX.X).then_inc(masked, 1)
                    dve.wait_ge(masked, n * 3 + 2)
                    nc.vector.reciprocal(den[:, 1:2], den[:, 0:1]).then_inc(masked, 1)
                    dve.wait_ge(turned, n + 1)
                    nc.vector.tensor_copy(et[:, :, :].rearrange("p k c -> p (k c)"),
                                          ps[:, 0:NT // CH, :].rearrange("p a c -> p (a c)")).then_inc(copied, 1)
                    dve.wait_ge(products, n + 1)
                    dve.wait_ge(masked, n * 3 + 3)
                    nc.vector.scalar_tensor_tensor(x1[:, :], ps[:, NT // CH, 0:D], den[:, 1:2], x1[:, :],
                                                   ALU.mult, ALU.add).then_inc(result, 1)

            where_wide(dve, batch)

        @block.tensor
        def _(pe):
            def batch(half, k):
                with pe.Fori(0, NT) as t:
                    n = (half * HB + k) * NT + t
                    pe.wait_ge(masked, n * 3 + 1)
                    for j in range(NT):
                        last = nc.tensor.transpose(ps[:, j // CH, P * (j % CH):P * (j % CH + 1)], e[:, P * j:P * (j + 1)],
                                                   ident[:, :])
                    last.then_inc(turned, 1)
                    pe.wait_ge(copied, n + 1)
                    for j in range(NT):
                        last = nc.tensor.matmul(ps[:, NT // CH, 0:D], et[:, j, :], g_all[:, j, 0:D],
                                                start=j == 0, stop=j == NT - 1)
                    last.then_inc(products, 1)

            pe.wait_ge(ident_made, 2)
            where_wide(pe, batch)


def build(nc, x, adj, theta, bias, gw, a_src, a_dst, out):
    pad_dram = nc.dram_tensor("pad", (2, DMA, D), F32).ap()
    z_dram = nc.dram_tensor("z_scratch", (2, 2, NT, P, W), F32).ap()
    mt_dram = nc.dram_tensor("mask_scratch", (NT, P, N), BF16).ap()
    x1_dram = nc.dram_tensor("x1_scratch", (2, NT, P, W), F32).ap()
    g_dram = nc.dram_tensor("g_scratch", (2, NT, P, HB * GE), F32).ap()
    ds_dram = nc.dram_tensor("ds_scratch", (2, 2 * HB * NT, P), F32).ap()
    with nc.sbuf_tensor("wide", [P, 1], I32) as wide:
        layers(nc, wide, x, adj, theta, bias, gw, a_src, a_dst, z_dram, mt_dram, x1_dram, g_dram, ds_dram, pad_dram, out)
        layer1_wide(nc, wide, adj, x1_dram, g_dram, ds_dram, out)


INPUTS = ["x", "adj", "L0_gnn_Theta1", "L0_gnn_bias", "L1_gnn_w", "L1_gnn_a_src", "L1_gnn_a_dst"]


def kernel(**inputs):
    import numpy as np
    import concourse.bacc as bacc
    from concourse.bass_utils import run_bass_kernel_spmd

    nc = bacc.Bacc("TRN2", target_bir_lowering=False, num_devices=1)
    arrays = {f"in_{n}": np.ascontiguousarray(inputs[n]) for n in INPUTS}
    aps = [nc.dram_tensor(n, a.shape, mybir.dt.from_np(a.dtype), kind="ExternalInput").ap() for n, a in arrays.items()]
    out = nc.dram_tensor("out", (B, N, D), F32, kind="ExternalOutput").ap()
    build(nc, *aps, out)
    return run_bass_kernel_spmd(nc, [arrays], core_ids=[0]).results[0]["out"]
```
